# Optimizing a Trainium2 kernel written in Bass

```python
import numpy as np
import jax
import jax.numpy as jnp

def _softmax(x, axis=-1):
    return jax.nn.softmax(x, axis=axis)

def _gelu(x):
    return jax.nn.gelu(x, approximate=True)

def _silu(x):
    return jax.nn.silu(x)

def _sigmoid(x):
    return jax.nn.sigmoid(x)

def _layernorm(x, axis=-1, eps=1e-05):
    m = jnp.mean(x, axis=axis, keepdims=True)
    v = jnp.var(x, axis=axis, keepdims=True)
    return (x - m) / jnp.sqrt(v + eps)

def _scatter_add(tgt, idx, src, axis=0):
    return tgt.at[idx].add(src)

def _segment_sum(src, seg, n):
    return jax.ops.segment_sum(src, seg, n)
kernel_name = 'mk_xattn_ffn_d4_seqx_r4_336dab'

def setup_inputs(seed: int=0):
    np.random.seed(seed)
    _w = jnp.asarray

    def _rec_inputs():
        import jax
        import jax.numpy as jnp
        _rk = jax.random.key(seed)
        x = 0.0003765 + 1 * jax.random.normal(jax.random.fold_in(_rk, 1), (2, 1024, 256), jnp.float32)
        _lenS = 1024 - jax.random.randint(jax.random.fold_in(_rk, 7), (2,), 0, max(1, 1024 // 4) + 1, jnp.int32)
        _lenS2 = 77 - jax.random.randint(jax.random.fold_in(_rk, 8), (2,), 0, max(1, 77 // 4) + 1, jnp.int32)
        _ctx_1024P = jax.random.normal(jax.random.fold_in(_rk, 11), (2, 16, 256), jnp.float32)
        _ctx_1024c = jax.random.dirichlet(jax.random.fold_in(_rk, 511), 0.3 * jnp.ones((16,), jnp.float32), (2, 77))
        _ctx_1024t = jnp.einsum('bsk,bkd->bsd', _ctx_1024c, _ctx_1024P)
        _ctx_1024t = _ctx_1024t * jax.lax.rsqrt(jnp.mean(jnp.square(_ctx_1024t)) + 1e-12) * 0.953939
        ctx_1024 = -0.000292821 + 1.00034 * (_ctx_1024t + 0.3 * jax.random.normal(jax.random.fold_in(_rk, 611), (2, 77, 256), jnp.float32))
        fside_BxSxS2_0 = jax.random.uniform(jax.random.fold_in(_rk, 15), (2, 1024, 77), jnp.float32, 0.0, 0.999998)
        _validS = jnp.arange(1024)[None, :] < _lenS[:, None]
        _validS2 = jnp.arange(77)[None, :] < _lenS2[:, None]
        _causal = jnp.tril(jnp.ones((1024, 1024), dtype=bool))
        mask_Bx1xSxS2_ik1 = jnp.where(jnp.broadcast_to(_validS2[:, None, None, :], (2, 1, 1024, 77)), 1, 0).astype(jnp.int32)
        mask_BxS_ff1 = jnp.where(jnp.ones((2, 1024), dtype=bool), 1.0, 0.0).astype(jnp.float32)
        mask_BxS2_ik0 = jnp.where(jnp.broadcast_to(_validS2[:, :], (2, 77)), 0, 1).astype(jnp.int32)
        mask_Bx1x1xS2_ff0 = jnp.where(jnp.ones((2, 1, 1, 77), dtype=bool), 0.0, -1000000000.0).astype(jnp.float32)
        return (x, ctx_1024, fside_BxSxS2_0, mask_Bx1xSxS2_ik1, mask_BxS_ff1, mask_BxS2_ik0, mask_Bx1x1xS2_ff0)
    x, ctx_1024, fside_BxSxS2_0, mask_Bx1xSxS2_ik1, mask_BxS_ff1, mask_BxS2_ik0, mask_Bx1x1xS2_ff0 = _rec_inputs()

    def _L0_xattn_setup():
        import jax, jax.numpy as jnp
        import numpy as np
        D_MODEL = 256
        HEADS = 16
        D_K = D_MODEL // HEADS
        NEG_INF = -10000000000.0
        key = jax.random.key(seed)
        ks = jax.random.split(key, 10)
        n, s = (2, 512)
        inp = {'value': jax.random.normal(ks[0], (n, s, D_MODEL), dtype=jnp.float32), 'key': jax.random.normal(ks[1], (n, s, D_MODEL), dtype=jnp.float32), 'query': jax.random.normal(ks[2], (n, s, D_MODEL), dtype=jnp.float32), 'mask': jax.random.randint(ks[3], (n, 1, s, s), 0, 2, dtype=jnp.int32), 'Wq': jax.random.normal(ks[4], (D_MODEL, D_MODEL), dtype=jnp.float32) * D_MODEL ** (-0.5), 'Wk': jax.random.normal(ks[5], (D_MODEL, D_MODEL), dtype=jnp.float32) * D_MODEL ** (-0.5), 'Wv': jax.random.normal(ks[6], (D_MODEL, D_MODEL), dtype=jnp.float32) * D_MODEL ** (-0.5), 'Wo': jax.random.normal(ks[7], (D_MODEL, D_MODEL), dtype=jnp.float32) * D_MODEL ** (-0.5), 'bo': jax.random.normal(ks[8], (D_MODEL,), dtype=jnp.float32) * 0.01}
        return inp
    _L0_xattn_all = _L0_xattn_setup()
    _L0_xattn_in = {k: v for k, v in _L0_xattn_all.items() if k in ('Wq', 'Wk', 'Wv', 'Wo', 'bo')}
    del _L0_xattn_all

    def _L0_ffn_setup():
        import jax, jax.numpy as jnp
        import numpy as np
        DIM = 256
        HIDDEN = 256
        NUM_EXPERTS = 8
        TOP_K = 2
        key = jax.random.key(seed)
        ks = jax.random.split(key, 8)
        std = 0.02
        x = jax.random.normal(ks[0], (2, 256, DIM), dtype=jnp.float32)
        gate_w = jax.random.normal(ks[1], (NUM_EXPERTS, DIM), dtype=jnp.float32) * std
        w1 = jax.random.normal(ks[2], (NUM_EXPERTS, DIM, HIDDEN), dtype=jnp.float32) * std
        w2 = jax.random.normal(ks[3], (NUM_EXPERTS, HIDDEN, DIM), dtype=jnp.float32) * std
        w3 = jax.random.normal(ks[4], (NUM_EXPERTS, DIM, HIDDEN), dtype=jnp.float32) * std
        w1s = jax.random.normal(ks[5], (1, DIM, HIDDEN), dtype=jnp.float32) * std
        w2s = jax.random.normal(ks[6], (1, HIDDEN, DIM), dtype=jnp.float32) * std
        w3s = jax.random.normal(ks[7], (1, DIM, HIDDEN), dtype=jnp.float32) * std
        return {'x': x, 'gate_w': gate_w, 'w1': w1, 'w2': w2, 'w3': w3, 'w1s': w1s, 'w2s': w2s, 'w3s': w3s}
    _L0_ffn_all = _L0_ffn_setup()
    _L0_ffn_in = {k: v for k, v in _L0_ffn_all.items() if k in ('gate_w', 'w1', 'w2', 'w3', 'w1s', 'w2s', 'w3s')}
    del _L0_ffn_all

    def _L1_xattn_setup():
        import jax, jax.numpy as jnp
        import numpy as np
        B, F, T, D = (8, 64, 32, 256)
        NEG = -1e+30
        key = jax.random.key(seed)
        ks = jax.random.split(key, 10)
        s = 1.0 / np.sqrt(D)
        return {'features': jax.random.normal(ks[0], (B, F, D), jnp.float32), 'masks': jnp.ones((B, F), jnp.float32), 'textual_features': jax.random.normal(ks[1], (B, T, D), jnp.float32), 'q_masks': jax.random.randint(ks[2], (B, T), 0, 2, jnp.int32), 'Ws': jax.random.normal(ks[3], (D, D), jnp.float32) * s, 'W': jax.random.normal(ks[4], (D, D), jnp.float32) * s, 'w': jax.random.normal(ks[5], (D, 1), jnp.float32) * s, 'b': jax.random.normal(ks[6], (1, D), jnp.float32) * s, 'Wcw': jax.random.normal(ks[7], (1, D), jnp.float32) * s, 'bcw': jnp.zeros((1,), jnp.float32), 'Wcb': jax.random.normal(ks[8], (1, D), jnp.float32) * s, 'bcb': jnp.zeros((1,), jnp.float32)}
    _L1_xattn_all = _L1_xattn_setup()
    _L1_xattn_in = {k: v for k, v in _L1_xattn_all.items() if k in ('Ws', 'W', 'w', 'b', 'Wcw', 'bcw', 'Wcb', 'bcb')}
    del _L1_xattn_all

    def _L1_ffn_setup():
        import jax, jax.numpy as jnp
        import numpy as np
        B, N, DIM = (2, 512, 256)
        HEADS, DIM_HEAD, EXPERTS = (8, 64, 8)
        SCALE = DIM_HEAD ** (-0.5)
        key = jax.random.key(seed)
        ks = jax.random.split(key, 6)
        dim_inner = HEADS * DIM_HEAD
        return {'x': jax.random.normal(ks[0], (B, N, DIM), jnp.float32), 'w_q': jax.random.normal(ks[1], (DIM, dim_inner), jnp.float32) * 0.02, 'w_k': jax.random.normal(ks[2], (DIM, dim_inner), jnp.float32) * 0.02, 'w_gate': jax.random.normal(ks[3], (DIM, HEADS * EXPERTS), jnp.float32) * 0.02, 'value_experts': jax.random.normal(ks[4], (EXPERTS, HEADS, DIM, DIM_HEAD), jnp.float32) * 0.02, 'output_experts': jax.random.normal(ks[5], (EXPERTS, HEADS, DIM_HEAD, DIM), jnp.float32) * 0.02}
    _L1_ffn_all = _L1_ffn_setup()
    _L1_ffn_in = {k: v for k, v in _L1_ffn_all.items() if k in ('w_q', 'w_k', 'w_gate', 'value_experts', 'output_experts')}
    del _L1_ffn_all

    def _L2_xattn_setup():
        import jax, jax.numpy as jnp
        import numpy as np
        B, F, T = (2, 128, 128)
        D, N, H = (256, 16, 64)
        K = 32
        FILT = 1024
        L = 4
        EPS = 1e-06

        def _glorot(key, shape, fan_in, fan_out):
            lim = np.sqrt(6.0 / (fan_in + fan_out)).astype(np.float32)
            return jax.random.uniform(key, shape, jnp.float32, -lim, lim)

        def _norm(x):
            m = jnp.mean(x, axis=-1, keepdims=True)
            s = jnp.sqrt(jnp.mean((x - m) ** 2, axis=-1, keepdims=True))
            return (x - m) / (s + EPS)

        def _attention(x, src, dist, bias, Wq, Wk, Wv, Wo, Wth, bth, Wto, bto):
            q = jnp.einsum('bfd,dnh->bfnh', x, Wq) * H ** (-0.5)
            k = jnp.einsum('btd,dnh->btnh', src, Wk)
            v = jnp.einsum('btd,dnh->btnh', src, Wv)
            hbias = jax.nn.relu(dist[..., None] @ Wth + bth)
            qs_bias = (hbias @ Wto + bto)[..., 0]
            logits = jnp.einsum('btnh,bfnh->bnft', k, q)
            logits = logits + bias + qs_bias[:, None]
            w = jax.nn.softmax(logits, axis=-1)
            out = jnp.einsum('bnft,btnh->bfnh', w, v)
            return jnp.einsum('bfnh,nhd->bfd', out, Wo)
        key = jax.random.key(seed)
        ks = jax.random.split(key, 18)
        inp = {'decoder_inputs': jax.random.normal(ks[0], (B, F, D), jnp.float32), 'encoder_outputs': jax.random.normal(ks[1], (B, T, D), jnp.float32), 'decoder_times_dist': jax.random.uniform(ks[2], (B, F, F), jnp.float32), 'decoder_encoder_times_dist': jax.random.uniform(ks[3], (B, F, T), jnp.float32), 'dec_self_attn_bias': jnp.zeros((B, 1, 1, F), jnp.float32), 'enc_dec_attn_bias': jnp.zeros((B, 1, 1, T), jnp.float32), 'Wq': _glorot(ks[4], (L, D, N, H), D, D), 'Wk': _glorot(ks[5], (L, D, N, H), D, D), 'Wv': _glorot(ks[6], (L, D, N, H), D, D), 'Wo': _glorot(ks[7], (L, N, H, D), D, D), 'Wth': _glorot(ks[8], (L, 1, K), 1, K), 'bth': jnp.zeros((L, K), jnp.float32), 'Wto': _glorot(ks[9], (L, K, 1), K, 1), 'bto': jnp.zeros((L, 1), jnp.float32), 'Wf1': _glorot(ks[10], (L, D, FILT), D, FILT), 'bf1': jnp.zeros((L, FILT), jnp.float32), 'Wf2': _glorot(ks[11], (L, FILT, D), FILT, D), 'bf2': jnp.zeros((L, D), jnp.float32)}
        return inp
    _L2_xattn_all = _L2_xattn_setup()
    _L2_xattn_in = {k: v for k, v in _L2_xattn_all.items() if k in ('Wq', 'Wk', 'Wv', 'Wo', 'Wth', 'bth', 'Wto', 'bto', 'Wf1', 'bf1', 'Wf2', 'bf2')}
    del _L2_xattn_all

    def _L2_ffn_setup():
        import jax, jax.numpy as jnp
        import numpy as np
        key = jax.random.key(seed)
        kx, kw = jax.random.split(key)
        x = jax.random.normal(kx, (32, 1024, 256), dtype=jnp.float32)
        weight = jax.random.normal(kw, (256, 256), dtype=jnp.float32) * 0.01
        return {'x': x, 'weight': weight}
    _L2_ffn_all = _L2_ffn_setup()
    _L2_ffn_in = {k: v for k, v in _L2_ffn_all.items() if k in ('weight',)}
    del _L2_ffn_all

    def _L3_xattn_setup():
        import jax, jax.numpy as jnp
        import numpy as np
        NOT_EPSILON = 1.0
        W_SCALE = 0.05
        H, T, A, C = (8, 256, 64, 64)

        def swishmax(x, axis):
            m = jnp.max(x, axis=axis, keepdims=True)
            xe = x * jnp.exp(x - m)
            return xe / (jnp.sum(jnp.abs(xe), axis=axis, keepdims=True) + NOT_EPSILON)
        key = jax.random.key(seed)
        ks = jax.random.split(key, 7)
        B, Q, K = (2, 512, 512)
        return {'query_tokens': jax.random.normal(ks[0], (B, Q, T), dtype=jnp.float32), 'key_tokens': jax.random.normal(ks[1], (B, K, T), dtype=jnp.float32), 'key_down': jax.random.normal(ks[2], (H, T, A), dtype=jnp.float32) * W_SCALE, 'query_down': jax.random.normal(ks[3], (H, T, A), dtype=jnp.float32) * W_SCALE, 'query_down_bias': jax.random.normal(ks[4], (H, 1, A), dtype=jnp.float32) * W_SCALE, 'value_down': jax.random.normal(ks[5], (H, T, C), dtype=jnp.float32) * W_SCALE, 'value_up': jax.random.normal(ks[6], (H, C, T), dtype=jnp.float32) * W_SCALE}
    _L3_xattn_all = _L3_xattn_setup()
    _L3_xattn_in = {k: v for k, v in _L3_xattn_all.items() if k in ('key_down', 'query_down', 'query_down_bias', 'value_down', 'value_up')}
    del _L3_xattn_all

    def _L3_ffn_setup():
        import jax, jax.numpy as jnp
        import numpy as np
        E, D, F, GATE_DIM = (8, 256, 1024, 16)
        B, T = (2, 512)
        key = jax.random.key(seed)
        ks = jax.random.split(key, 7)
        s = 0.02
        return {'hidden_states': jax.random.normal(ks[0], (B, T, D), dtype=jnp.float32), 'w_red': jax.random.normal(ks[1], (D, GATE_DIM), dtype=jnp.float32) * s, 'wg': jax.random.normal(ks[2], (E, GATE_DIM), dtype=jnp.float32), 'w1': jax.random.normal(ks[3], (E, D, F), dtype=jnp.float32) * s, 'b1': jax.random.normal(ks[4], (E, F), dtype=jnp.float32) * s, 'w2': jax.random.normal(ks[5], (E, F, D), dtype=jnp.float32) * s, 'b2': jax.random.normal(ks[6], (E, D), dtype=jnp.float32) * s}
    _L3_ffn_all = _L3_ffn_setup()
    _L3_ffn_in = {k: v for k, v in _L3_ffn_all.items() if k in ('w_red', 'wg', 'w1', 'b1', 'w2', 'b2')}
    del _L3_ffn_all
    return {'x': x, 'ctx_1024': ctx_1024, 'fside_BxSxS2_0': fside_BxSxS2_0, 'mask_Bx1xSxS2_ik1': mask_Bx1xSxS2_ik1, 'mask_BxS_ff1': mask_BxS_ff1, 'mask_BxS2_ik0': mask_BxS2_ik0, 'mask_Bx1x1xS2_ff0': mask_Bx1x1xS2_ff0, 'L0_xattn_Wq': _L0_xattn_in['Wq'], 'L0_xattn_Wk': _L0_xattn_in['Wk'], 'L0_xattn_Wv': _L0_xattn_in['Wv'], 'L0_xattn_Wo': _L0_xattn_in['Wo'], 'L0_xattn_bo': _L0_xattn_in['bo'], 'L0_ffn_gate_w': _L0_ffn_in['gate_w'], 'L0_ffn_w1': _L0_ffn_in['w1'], 'L0_ffn_w2': _L0_ffn_in['w2'], 'L0_ffn_w3': _L0_ffn_in['w3'], 'L0_ffn_w1s': _L0_ffn_in['w1s'], 'L0_ffn_w2s': _L0_ffn_in['w2s'], 'L0_ffn_w3s': _L0_ffn_in['w3s'], 'L1_xattn_Ws': _L1_xattn_in['Ws'], 'L1_xattn_W': _L1_xattn_in['W'], 'L1_xattn_w': _L1_xattn_in['w'], 'L1_xattn_b': _L1_xattn_in['b'], 'L1_xattn_Wcw': _L1_xattn_in['Wcw'], 'L1_xattn_bcw': _L1_xattn_in['bcw'], 'L1_xattn_Wcb': _L1_xattn_in['Wcb'], 'L1_xattn_bcb': _L1_xattn_in['bcb'], 'L1_ffn_w_q': _L1_ffn_in['w_q'], 'L1_ffn_w_k': _L1_ffn_in['w_k'], 'L1_ffn_w_gate': _L1_ffn_in['w_gate'], 'L1_ffn_value_experts': _L1_ffn_in['value_experts'], 'L1_ffn_output_experts': _L1_ffn_in['output_experts'], 'L2_xattn_Wq': _L2_xattn_in['Wq'], 'L2_xattn_Wk': _L2_xattn_in['Wk'], 'L2_xattn_Wv': _L2_xattn_in['Wv'], 'L2_xattn_Wo': _L2_xattn_in['Wo'], 'L2_xattn_Wth': _L2_xattn_in['Wth'], 'L2_xattn_bth': _L2_xattn_in['bth'], 'L2_xattn_Wto': _L2_xattn_in['Wto'], 'L2_xattn_bto': _L2_xattn_in['bto'], 'L2_xattn_Wf1': _L2_xattn_in['Wf1'], 'L2_xattn_bf1': _L2_xattn_in['bf1'], 'L2_xattn_Wf2': _L2_xattn_in['Wf2'], 'L2_xattn_bf2': _L2_xattn_in['bf2'], 'L2_ffn_weight': _L2_ffn_in['weight'], 'L3_xattn_key_down': _L3_xattn_in['key_down'], 'L3_xattn_query_down': _L3_xattn_in['query_down'], 'L3_xattn_query_down_bias': _L3_xattn_in['query_down_bias'], 'L3_xattn_value_down': _L3_xattn_in['value_down'], 'L3_xattn_value_up': _L3_xattn_in['value_up'], 'L3_ffn_w_red': _L3_ffn_in['w_red'], 'L3_ffn_wg': _L3_ffn_in['wg'], 'L3_ffn_w1': _L3_ffn_in['w1'], 'L3_ffn_b1': _L3_ffn_in['b1'], 'L3_ffn_w2': _L3_ffn_in['w2'], 'L3_ffn_b2': _L3_ffn_in['b2']}

def reference(x, ctx_1024, fside_BxSxS2_0, mask_Bx1xSxS2_ik1, mask_BxS_ff1, mask_BxS2_ik0, mask_Bx1x1xS2_ff0, L0_xattn_Wq, L0_xattn_Wk, L0_xattn_Wv, L0_xattn_Wo, L0_xattn_bo, L0_ffn_gate_w, L0_ffn_w1, L0_ffn_w2, L0_ffn_w3, L0_ffn_w1s, L0_ffn_w2s, L0_ffn_w3s, L1_xattn_Ws, L1_xattn_W, L1_xattn_w, L1_xattn_b, L1_xattn_Wcw, L1_xattn_bcw, L1_xattn_Wcb, L1_xattn_bcb, L1_ffn_w_q, L1_ffn_w_k, L1_ffn_w_gate, L1_ffn_value_experts, L1_ffn_output_experts, L2_xattn_Wq, L2_xattn_Wk, L2_xattn_Wv, L2_xattn_Wo, L2_xattn_Wth, L2_xattn_bth, L2_xattn_Wto, L2_xattn_bto, L2_xattn_Wf1, L2_xattn_bf1, L2_xattn_Wf2, L2_xattn_bf2, L2_ffn_weight, L3_xattn_key_down, L3_xattn_query_down, L3_xattn_query_down_bias, L3_xattn_value_down, L3_xattn_value_up, L3_ffn_w_red, L3_ffn_wg, L3_ffn_w1, L3_ffn_b1, L3_ffn_w2, L3_ffn_b2):
    import jax
    import jax.numpy as jnp

    def _L0_xattn_ref(value, key, query, mask, Wq, Wk, Wv, Wo, bo):
        import jax, jax.numpy as jnp
        import numpy as np
        D_MODEL = 256
        HEADS = 16
        D_K = D_MODEL // HEADS
        NEG_INF = -10000000000.0
        n, q_len, _ = query.shape
        q = (query @ Wq.T).reshape(n, q_len, HEADS, D_K)
        k = (key @ Wk.T).reshape(n, key.shape[1], HEADS, D_K)
        v = (value @ Wv.T).reshape(n, value.shape[1], HEADS, D_K)
        scores = jnp.einsum('nqhd,nkhd->nhqk', q, k)
        scores = jnp.where(mask == 0, jnp.float32(NEG_INF), scores)
        attn = jax.nn.softmax(scores / jnp.sqrt(jnp.float32(D_K)), axis=-1)
        out = jnp.einsum('nhql,nlhd->nqhd', attn, v).reshape(n, q_len, D_MODEL)
        return out @ Wo.T + bo

    def _L0_ffn_ref(x, gate_w, w1, w2, w3, w1s, w2s, w3s):
        import jax, jax.numpy as jnp
        import numpy as np
        DIM = 256
        HIDDEN = 256
        NUM_EXPERTS = 8
        TOP_K = 2
        bs, slen, dim = x.shape
        xt = x.reshape(bs * slen, dim)
        logits = xt @ gate_w.T
        scores = jax.nn.softmax(logits.astype(jnp.float32), axis=1).astype(x.dtype)
        top_scores, sel = jax.lax.top_k(scores, TOP_K)
        sel_flat = sel.reshape(-1)
        order = jnp.argsort(sel_flat, stable=True)
        top_scores_sorted = top_scores.reshape(-1)[order]
        token_idx = order // TOP_K
        eid = sel_flat[order]
        routed_in = xt[token_idx] * top_scores_sorted[:, None]
        out_routed = jnp.zeros_like(routed_in)
        for e in range(NUM_EXPERTS):
            m = (eid == e)[:, None]
            xe = jnp.where(m, routed_in, 0.0)
            h = jax.nn.silu(xe @ w1[e]) * (xe @ w3[e])
            out_routed = out_routed + jnp.where(m, h @ w2[e], 0.0)
        hs = jax.nn.silu(xt @ w1s[0]) * (xt @ w3s[0])
        out = hs @ w2s[0]
        out = out.at[token_idx].add(out_routed)
        return out.reshape(bs, slen, dim)

    def _L1_xattn_ref(features, masks, textual_features, q_masks, Ws, W, w, b, Wcw, bcw, Wcb, bcb):
        import jax, jax.numpy as jnp
        import numpy as np
        B, F, T, D = (8, 64, 32, 256)
        NEG = -1e+30
        txt_proj = jnp.einsum('btd,de->bte', textual_features, Ws)
        feat_proj = jnp.einsum('bfd,de->bfe', features, W)
        h = jnp.tanh(txt_proj[:, None, :, :] + feat_proj[:, :, None, :] + b[None, None, :, :][..., 0, :])
        rho = jnp.einsum('bftd,d->bft', h, w[:, 0])
        qm = q_masks.astype(jnp.float32)
        rho = rho + (1.0 - qm)[:, None, :] * NEG
        att = jax.nn.softmax(rho, axis=-1)
        txt_h = jnp.einsum('bft,btd->bfd', att, textual_features)
        w_s = jnp.tanh(jnp.einsum('bfd,od->bfo', txt_h, Wcw) + bcw)
        b_s = jnp.tanh(jnp.einsum('bfd,od->bfo', txt_h, Wcb) + bcb)
        return w_s * features + b_s

    def _L1_ffn_ref(x, w_q, w_k, w_gate, value_experts, output_experts):
        import jax, jax.numpy as jnp
        import numpy as np
        B, N, DIM = (2, 512, 256)
        HEADS, DIM_HEAD, EXPERTS = (8, 64, 8)
        SCALE = DIM_HEAD ** (-0.5)
        b, n, _ = x.shape
        q = (x @ w_q).reshape(b, n, HEADS, DIM_HEAD).transpose(0, 2, 1, 3)
        k = (x @ w_k).reshape(b, n, HEADS, DIM_HEAD).transpose(0, 2, 1, 3)
        gates = jax.nn.sigmoid((x @ w_gate).reshape(b, n, HEADS, EXPERTS).transpose(0, 2, 1, 3))
        sel = jnp.argmax(gates, axis=-1)
        gm = jax.nn.one_hot(sel, EXPERTS, dtype=x.dtype) * gates
        values = jnp.einsum('bhne,ehdk,bnd->bhnk', gm, value_experts, x)
        sim = jnp.einsum('bhid,bhjd->bhij', q * SCALE, k)
        causal_mask = jnp.triu(jnp.ones((n, n), dtype=bool), 1)
        sim = jnp.where(causal_mask, jnp.finfo(sim.dtype).min, sim)
        attn = jax.nn.softmax(sim, axis=-1)
        out = jnp.einsum('bhij,bhjk->bhik', attn, values)
        out = jnp.einsum('bhne,ehkd,bhnk->bhnd', gm, output_experts, out)
        return out.sum(axis=1)

    def _L2_xattn_ref(decoder_inputs, encoder_outputs, decoder_times_dist, decoder_encoder_times_dist, dec_self_attn_bias, enc_dec_attn_bias, Wq, Wk, Wv, Wo, Wth, bth, Wto, bto, Wf1, bf1, Wf2, bf2):
        import jax, jax.numpy as jnp
        import numpy as np
        B, F, T = (2, 128, 128)
        D, N, H = (256, 16, 64)
        K = 32
        FILT = 1024
        L = 4
        EPS = 1e-06

        def _glorot(key, shape, fan_in, fan_out):
            lim = np.sqrt(6.0 / (fan_in + fan_out)).astype(np.float32)
            return jax.random.uniform(key, shape, jnp.float32, -lim, lim)

        def _norm(x):
            m = jnp.mean(x, axis=-1, keepdims=True)
            s = jnp.sqrt(jnp.mean((x - m) ** 2, axis=-1, keepdims=True))
            return (x - m) / (s + EPS)

        def _attention(x, src, dist, bias, Wq, Wk, Wv, Wo, Wth, bth, Wto, bto):
            q = jnp.einsum('bfd,dnh->bfnh', x, Wq) * H ** (-0.5)
            k = jnp.einsum('btd,dnh->btnh', src, Wk)
            v = jnp.einsum('btd,dnh->btnh', src, Wv)
            hbias = jax.nn.relu(dist[..., None] @ Wth + bth)
            qs_bias = (hbias @ Wto + bto)[..., 0]
            logits = jnp.einsum('btnh,bfnh->bnft', k, q)
            logits = logits + bias + qs_bias[:, None]
            w = jax.nn.softmax(logits, axis=-1)
            out = jnp.einsum('bnft,btnh->bfnh', w, v)
            return jnp.einsum('bfnh,nhd->bfd', out, Wo)
        x = decoder_inputs
        for i in range(L):
            y = _attention(_norm(x), encoder_outputs, decoder_encoder_times_dist, enc_dec_attn_bias, Wq[i], Wk[i], Wv[i], Wo[i], Wth[i], bth[i], Wto[i], bto[i])
            x = x + y
            y = jax.nn.relu(_norm(x) @ Wf1[i] + bf1[i]) @ Wf2[i] + bf2[i]
            x = x + y
        return _norm(x)

    def _L2_ffn_ref(x, weight):
        import jax, jax.numpy as jnp
        import numpy as np
        b_weight = jnp.sign(weight)
        return jnp.einsum('bsi,oi->bso', x, b_weight)

    def _L3_xattn_ref(query_tokens, key_tokens, key_down, query_down, query_down_bias, value_down, value_up):
        import jax, jax.numpy as jnp
        import numpy as np
        NOT_EPSILON = 1.0
        W_SCALE = 0.05
        H, T, A, C = (8, 256, 64, 64)

        def swishmax(x, axis):
            m = jnp.max(x, axis=axis, keepdims=True)
            xe = x * jnp.exp(x - m)
            return xe / (jnp.sum(jnp.abs(xe), axis=axis, keepdims=True) + NOT_EPSILON)
        k = jnp.einsum('bkt,hta->bhka', key_tokens, key_down)
        q = jnp.einsum('bqt,hta->bhqa', query_tokens, query_down) + query_down_bias[None]
        logits = jnp.einsum('bhka,bhqa->bhkq', k, q)
        attn = swishmax(logits, axis=-2)
        vs = jnp.einsum('bhkq,bkt->bhqt', attn, key_tokens)
        vs = jnp.einsum('bhqc,hct->bhqt', jnp.einsum('bhqt,htc->bhqc', vs, value_down), value_up)
        return vs.sum(axis=1)

    def _L3_ffn_ref(hidden_states, w_red, wg, w1, b1, w2, b2):
        import jax, jax.numpy as jnp
        import numpy as np
        E, D, F, GATE_DIM = (8, 256, 1024, 16)
        B, T = (2, 512)
        b, t, c = hidden_states.shape
        x = hidden_states.reshape(-1, c)
        red = x @ w_red
        wg_n = wg / jnp.maximum(jnp.linalg.norm(wg, axis=1, keepdims=True), 0.0001)
        logits = red @ wg_n.T
        gates = jax.nn.softmax(logits, axis=1)
        idx = jnp.argmax(gates, axis=1)
        scores = jnp.take_along_axis(gates, idx[:, None], axis=1)
        h = jax.nn.gelu(jnp.einsum('td,edf->etf', x, w1) + b1[:, None, :], approximate=False)
        y = jnp.einsum('etf,efd->etd', h, w2) + b2[:, None, :]
        out = jnp.take_along_axis(y, idx[None, :, None], axis=0)[0]
        out = out * scores
        return out.reshape(b, t, c)
    x = x + _L0_xattn_ref(ctx_1024, ctx_1024, _layernorm(x, axis=-1), mask_Bx1xSxS2_ik1, L0_xattn_Wq, L0_xattn_Wk, L0_xattn_Wv, L0_xattn_Wo, L0_xattn_bo)
    x = x + _L0_ffn_ref(_layernorm(x, axis=-1), L0_ffn_gate_w, L0_ffn_w1, L0_ffn_w2, L0_ffn_w3, L0_ffn_w1s, L0_ffn_w2s, L0_ffn_w3s)
    x = x + _L1_xattn_ref(_layernorm(x, axis=-1), mask_BxS_ff1, ctx_1024, mask_BxS2_ik0, L1_xattn_Ws, L1_xattn_W, L1_xattn_w, L1_xattn_b, L1_xattn_Wcw, L1_xattn_bcw, L1_xattn_Wcb, L1_xattn_bcb)
    x = x + _L1_ffn_ref(_layernorm(x, axis=-1), L1_ffn_w_q, L1_ffn_w_k, L1_ffn_w_gate, L1_ffn_value_experts, L1_ffn_output_experts)
    x = x + _L2_xattn_ref(_layernorm(x, axis=-1), ctx_1024, fside_BxSxS2_0, fside_BxSxS2_0, mask_Bx1x1xS2_ff0, mask_Bx1x1xS2_ff0, L2_xattn_Wq, L2_xattn_Wk, L2_xattn_Wv, L2_xattn_Wo, L2_xattn_Wth, L2_xattn_bth, L2_xattn_Wto, L2_xattn_bto, L2_xattn_Wf1, L2_xattn_bf1, L2_xattn_Wf2, L2_xattn_bf2)
    x = x + _L2_ffn_ref(_layernorm(x, axis=-1), L2_ffn_weight)
    x = x + _L3_xattn_ref(_layernorm(x, axis=-1), ctx_1024, L3_xattn_key_down, L3_xattn_query_down, L3_xattn_query_down_bias, L3_xattn_value_down, L3_xattn_value_up)
    x = x + _L3_ffn_ref(_layernorm(x, axis=-1), L3_ffn_w_red, L3_ffn_wg, L3_ffn_w1, L3_ffn_b1, L3_ffn_w2, L3_ffn_b2)
    return x

_drawn_inputs = setup_inputs


def setup_inputs(seed=0):
    import zlib

    import numpy as np

    out = dict(_drawn_inputs(seed))
    spreads = {'L2_xattn_bth': (0.0, 2.0),
     'L2_xattn_bto': (0.0, 2.0),
     'L2_xattn_bf1': (0.0, 0.377),
     'L2_xattn_bf2': (0.0, 0.392)}
    factors = {'fside_BxSxS2_0': 6.754,
     'L0_xattn_bo': 7.079,
     'L0_ffn_gate_w': 8.0,
     'L0_ffn_w1': 8.0,
     'L0_ffn_w2': 8.0,
     'L0_ffn_w3': 8.0,
     'L0_ffn_w1s': 3.821,
     'L0_ffn_w2s': 3.738,
     'L0_ffn_w3s': 3.969,
     'L1_xattn_W': 3.903,
     'L1_xattn_w': 3.403,
     'L1_xattn_b': 28.037,
     'L1_ffn_w_q': 8.0,
     'L1_ffn_w_k': 8.0,
     'L1_ffn_w_gate': 7.993,
     'L1_ffn_value_experts': 7.781,
     'L1_ffn_output_experts': 7.78,
     'L2_xattn_Wth': 7.701,
     'L2_xattn_Wto': 5.568,
     'L3_xattn_query_down_bias': 8.0,
     'L3_ffn_w_red': 8.0,
     'L3_ffn_wg': 8.0,
     'L3_ffn_w1': 8.0,
     'L3_ffn_b1': 22.315,
     'L3_ffn_w2': 8.0,
     'L3_ffn_b2': 64.0}
    for name, (base, spread) in spreads.items():
        noise = np.random.default_rng([zlib.crc32(name.encode()), seed]).standard_normal(out[name].shape)
        drawn = base * np.exp(spread * noise) if base else spread * noise
        out[name] = jnp.asarray(drawn.astype(out[name].dtype))
    for name, factor in factors.items():
        out[name] = (out[name] * factor).astype(out[name].dtype)
    return out
```

```python
import concourse.bass as bass
from concourse import mybir
from contextlib import ExitStack

FP32 = mybir.dt.float32
INT32 = mybir.dt.int32
ALU = mybir.AluOpType
ACT = mybir.ActivationFunctionType
AXX = mybir.AxisListType.X

B, S, D, KEYS = 2, 1024, 256, 77
P = 128
KC = D // P
TILES = B * S // P
GROUPS = TILES // 4
GT = 4 * P
SLOT_TILES = 40
LAYERS = 4
HID = 1024
EXPERTS = 8
STOP_AFTER = 8


class CtxAttention:

    def __init__(self, heads, width, scale, kind):
        self.heads, self.width, self.scale, self.kind = heads, width, scale, kind
        self.chunks = width // P
        self.hpc = heads // self.chunks
        self.cols = heads * KEYS
        self.rows = -(-self.cols // P)
        self.tail = self.cols - P * (self.rows - 1)
        self.hpb = min(6, heads)
        self.halves = self.hpc * KEYS * B // 308
        self.a_units = self.chunks * self.halves * KC
        self.b_units = B * heads
        full, rest = divmod(heads, self.hpb)
        self.runs = [(0, full, self.hpb)] + ([(full, 1, rest)] if rest else [])


class Experts:

    def __init__(self, index, tiles, hid, kind, base, stored, loaded):
        self.index, self.tiles, self.hid, self.kind, self.base = index, tiles, hid, kind, base
        self.stored, self.loaded = stored, loaded
        self.up = 512 * (2 if kind == "gelu" else 1)
        self.chunks = hid // P


SHARED = Experts(0, 16, 256, "shared", 0, 0, 0)
SWIGLU = Experts(0, 40, 256, "swiglu", 16, 0, 0)
GELU = Experts(1, 24, 1024, "gelu", 56, 40, 40)

MASKED = CtxAttention(16, 256, 0.25, "masked")
TIMED = CtxAttention(16, 1024, 64 ** -0.5, "timed")
SWISH = CtxAttention(8, 512, 1.0, "swish")


def megakernel(nc, a, out):
    ctx = ExitStack()
    with ctx:
        def sem(name):
            return ctx.enter_context(nc.semaphore(name))

        arena = ctx.enter_context(nc.sbuf_tensor("arena", [P, 52000], FP32))
        ps = ctx.enter_context(nc.psum_tensor("ps", [P, 8, 512], FP32))
        scratch_b = nc.dram_tensor("scratch_b", [B, 16 * KEYS, D], FP32).ap()
        scores_dram = nc.dram_tensor("scores_dram", [KEYS, B * S], FP32).ap()
        slots_x = [nc.dram_tensor(f"slots_x{n}", [run.tiles * P, D], FP32).ap() for n, run in enumerate((SWIGLU, GELU))]
        slots_y = [nc.dram_tensor(f"slots_y{n}", [run.tiles * P, D], FP32).ap() for n, run in enumerate((SWIGLU, GELU))]

        top = [0]

        def region(size):
            off = top[0]
            top[0] += size
            assert top[0] <= 52000, top[0]
            return off

        def view(off, *dims):
            n = 1
            for d in dims:
                n *= d
            v = arena[:, off:off + n]
            if len(dims) == 1:
                return v
            names = "abcde"[:len(dims)]
            return v.rearrange("p (" + " ".join(names) + ") -> p " + " ".join(names),
                               **{m: d for m, d in zip(names[1:], dims[1:])})

        x = view(region(TILES * D), TILES, D)
        z = view(region(TILES * D), TILES, D)
        xn = view(region(2 * D), 2, D)
        xnT = view(region(2 * KC * P), 2, KC, P)
        xng = view(region(4 * D), 4, D)
        ident = view(region(P), P)
        tri = view(region(P), P)
        ctxT = view(region(KC * B * KEYS), KC, B * KEYS)
        bd_mask = view(region(10), 10)
        earlier = view(region(64), 8, 8)
        zero_row = view(region(D), D)
        later8 = view(region(8), 8)
        stats = view(region(16 * 6), 16, 6)
        mv = view(region(32), 16, 2)
        mv4 = view(region(8), 4, 2)
        rstd = view(region(16), 16)
        pow_in = view(region(16), 16)
        minus_half = view(region(16), 16)
        plus_half = view(region(16), 16)
        cols = view(region(512), 512)
        BASE = top[0]

        aw_off = region(4 * 8 * D)
        w_k = view(aw_off, KC, HID)
        w_v = view(aw_off + 2048, KC, HID)
        w_q = view(aw_off + 4096, 8, D)
        w_o = view(aw_off + 6144, 8, D)
        fold_q = view(region(KC * B * 1232), KC, B, 1232)
        fold_v = view(region(B * 10 * D), B, 10, D)
        bd_off = region(2 * B * 616)
        main_off = region(B * 16 * D)
        fold_v_rows = view(main_off, B, 16, D)
        shifted = view(main_off, 2, 1232)
        probs = view(main_off + 2464, 2, 1232)
        probsT = view(main_off + 4928, 2, 10, P)
        mx = view(region(32), 2, 16)
        rsum = view(region(32), 2, 16)
        rinv = view(region(32), 2, 16)
        dist = view(region(1232), 1232)
        qbias = view(region(1232), 1232)
        ff0 = view(region(B * KEYS), B * KEYS)
        cols_bo = view(region(D), D)
        head_bias_rep = view(region(4 * P), 4, P)
        head_bias = view(region(4), 4)
        ATT_END = top[0]
        relu_ring = view(region(2 * 1232), 2, 1232)
        tb = view(region(97), 97)
        keep = dist.rearrange("p (t k) -> p t k", k=KEYS)
        negm = qbias.rearrange("p (t k) -> p t k", k=KEYS)
        mask_i = relu_ring[:, 0, :].bitcast(INT32)
        raw_logits = relu_ring[:, :, 0:616]
        cbias = dist.rearrange("p (b k) -> p b k", b=B)
        w_f1 = view(region(KC * HID), KC, HID)
        w_f2 = view(region(8 * D), 8, D)
        b_f1 = view(region(8), 8)
        b_f2 = view(region(D), D)
        hidT = view(main_off, 8, GT)
        gT = view(main_off + 8 * GT, 2, KC, GT)
        
        over = [BASE]

        def overlay(size):
            off = over[0]
            over[0] += size
            assert over[0] <= 52000, over[0]
            return off

        before = view(overlay(P), P)
        ones = view(overlay(P), P)
        route = [view(overlay(P), TILES, EXPERTS) for _ in range(8)]
        tile_of = view(overlay(SLOT_TILES), SLOT_TILES)
        tile_expert_f = view(overlay(SLOT_TILES * EXPERTS), SLOT_TILES, EXPERTS)
        tile_expert = view(overlay(SLOT_TILES), SLOT_TILES).bitcast(INT32)
        tile_of_expert = view(overlay(SLOT_TILES), SLOT_TILES)
        slot_f = view(overlay(2 * TILES), 2, TILES)
        slot_i = view(overlay(2 * TILES), 2, TILES).bitcast(INT32)
        score = view(overlay(2 * TILES), 2, TILES)
        rcol = view(overlay(3 * TILES), 3, TILES)
        small8 = view(overlay(6 * EXPERTS), 6, EXPERTS)
        w_router = view(overlay(KC * 8), KC, 8)
        w_redT = view(overlay(D), D)[0:16, :]
        wg = view(overlay(16), 16)[0:8, :]
        wg_sq = view(overlay(16), 16)[0:8, :]
        wg_col = view(overlay(4), 4)[0:8, :]
        wgT = view(overlay(8), 8)[0:16, :]
        ff_h_swiglu = view(overlay(2 * 768), 2, 768)
        z_off = TILES * D
        ff_h_gelu = view(z_off, 2, HID)
        ff_b1 = view(z_off + 2 * HID, 2, HID)
        ff_hT = view(overlay(2 * HID), 2, HID)
        ff_y = view(overlay(2 * D), 2, D)
        pairT = ff_hT.rearrange("p a n -> p (a n)")[:, 0:2 * KC * 2 * P].rearrange("p (a k n) -> p a k n", a=2, k=KC)
        ff_b2 = view(overlay(2 * D), 2, D)
        rows_ring = view(overlay(2 * D), 2, D)
        ff_top = over[0]
        w13 = view(overlay(9 * KC * 512), 9, KC, 512)
        w2e = view(overlay(9 * KC * D), 9, KC, D)
        over[0] = ff_top

        w1g = view(overlay(EXPERTS * KC * HID), EXPERTS, KC, HID)
        w2g = view(overlay(EXPERTS * 8 * D), EXPERTS, 8, D)
        over[0] = BASE
        featT = view(overlay(KC * B * S), KC, B, S)
        tanhT = view(overlay(2 * B * KC * S), 2, B, KC, S)
        w_col = view(overlay(KC * 32), KC, 32)
        score_rows = view(overlay(2 * GT), 2, GT)
        rho_rows = view(overlay(B * S), B, S)[0:KEYS]
        textT = view(overlay(KC * B * KEYS), KC, B * KEYS)
        w_text = view(overlay(KC * D), KC, D)
        w_feat = view(overlay(KC * D), KC, D)
        gate_cols = view(overlay(8), 8)
        add_bias = view(overlay(2), 2)
        scal_bias = view(overlay(2), 2)
        gate_rep = view(overlay(2 * KC * P), 2, KC, P)
        gate_txt = view(overlay(2 * B * KEYS), 2, B * KEYS)
        q_mask_i = view(overlay(B * KEYS), B * KEYS).bitcast(INT32)
        q_mask = view(overlay(B * KEYS), B * KEYS)
        rho = view(overlay(TILES * KEYS), TILES, KEYS)
        rho2 = view(overlay(TILES * KEYS), TILES, KEYS)
        fcol = view(overlay(6 * TILES), 6, TILES)
        pairT2 = view(overlay(2 * KC * 2 * P), 2, KC, 2 * P)
        add_tmp = view(overlay(2 * D), 2, D)
        over[0] = BASE
        xnT_all = view(overlay(KC * TILES * P), KC, TILES * P)
        w_gate = view(overlay(KC * 64), KC, 64)
        gates = view(overlay(TILES * 64), TILES * 8, 8)
        gsel = view(overlay(TILES * 64), TILES * 8, 8)
        gpeak = view(overlay(2 * P), 2, P)
        pair_gates = view(overlay(TILES * 16), TILES, 16)
        w_qk = view(overlay(KC * 2 * P), KC, 2, P)
        w_ve = view(overlay(KC * 2 * 512), KC, 2, 512)
        w_oe = view(overlay(2 * 4 * D), 2, 4, D)
        QT = view(overlay(B * S), B, S)
        KT = view(overlay(B * S), B, S)
        V = view(overlay(TILES * P), TILES, 2, 64)
        v_tmp = view(overlay(2 * 512), 2, 8, 64)
        P_sb = view(overlay(2 * S), 2, S)
        PT_sb = view(overlay(2 * S), 2, 8, P)
        G_sb = view(overlay(2 * 512), 2, 512)
        GT_sb = view(overlay(2 * 512), 2, 4, P)
        acol = view(overlay(2 * 16), 2, 16)
        over[0] = BASE
        w_raw = view(overlay(KC * D), KC, D)
        w_sign = view(overlay(KC * D), KC, D)
        w_neg = view(overlay(KC * D), KC, D)
        pairT3 = view(overlay(2 * KC * 2 * P), 2, KC, 2 * P)
        over[0] = BASE

        consts_in = sem("consts_in")
        x_in = sem("x_in")
        out_stored = sem("out_stored")
        end_pe, end_act, end_dve, end_pool = (sem(f"end_{e}") for e in ("pe", "act", "dve", "pool"))
        end_sp = sem("end_sp")
        ends = {"pe": end_pe, "act": end_act, "dve": end_dve, "pool": end_pool}
        consts_made = sem("consts_made")
        zeros_made = sem("zeros_made")
        var_ready = sem("var_ready")
        rstd_ready = sem("rstd_ready")
        xn_ready = sem("xn_ready")
        xnT_psum = sem("xnT_psum")
        xnT_ready = sem("xnT_ready")
        all_var_ready = sem("all_var_ready")
        all_rstd_ready = sem("all_rstd_ready")
        att_w_in = sem("att_w_in")
        mask_in = sem("mask_in")
        bd_psum = sem("bd_psum")
        bd_ready = sem("bd_ready")
        fold_psum = sem("fold_psum")
        fold_ready = sem("fold_ready")
        fold_v_saved = sem("fold_v_saved")
        fold_v_in = sem("fold_v_in")
        logits_ready = sem("logits_ready")
        shifted_ready = sem("shifted_ready")
        exp_ready = sem("exp_ready")
        rinv_ready = sem("rinv_ready")
        probs_ready = sem("probs_ready")
        probsT_psum = sem("probsT_psum")
        probsT_ready = sem("probsT_ready")
        att_out = sem("att_out")
        x_updated = sem("x_updated")
        relu_ready = sem("relu_ready")
        relu_used = sem("relu_used")

        zeroed = sem("zeroed")
        route_consts_in = sem("route_consts_in")
        expert_landed = [sem(f"expert_landed{e}") for e in range(9)]
        experts_in = sem("experts_in")
        gelu_landed = [sem(f"gelu_landed{e}") for e in range(8)]
        wg_square = sem("wg_square")
        wg_norm = sem("wg_norm")
        wg_ready = sem("wg_ready")
        wgT_psum = sem("wgT_psum")
        wgT_ready = sem("wgT_ready")
        w_router_psum = sem("w_router_psum")
        w_router_ready = sem("w_router_ready")
        all_xn_ready = sem("all_xn_ready")
        rt_psum = sem("rt_psum")
        rt_ready = sem("rt_ready")
        router_ready = sem("router_ready")
        router_shifted = sem("router_shifted")
        router_exp = sem("router_exp")
        chosen_ready = sem("chosen_ready")
        ranks_ready = sem("ranks_ready")
        slots_ready = sem("slots_ready")
        row_scaled = sem("row_scaled")
        row_scattered = [sem(f"row_scattered{k}") for k in range(2)]
        row_gathered = [sem(f"row_gathered{k}") for k in range(2)]
        row_added = sem("row_added")
        ff_x_in = [sem(f"ff_x_in{k}") for k in range(2)]
        ff_x_handed = sem("ff_x_handed")
        ff_xT_psum = sem("ff_xT_psum")
        ff_xT_ready = sem("ff_xT_ready")
        ff_up = sem("ff_up")
        ff_gate = sem("ff_gate")
        ff_biased = sem("ff_biased")
        ff_h_ready = sem("ff_h_ready")
        ff_hT_psum = sem("ff_hT_psum")
        ff_hT_ready = sem("ff_hT_ready")
        ff_y_psum = sem("ff_y_psum")
        ff_y_ready = sem("ff_y_ready")
        ff_y_stored = [sem(f"ff_y_stored{k}") for k in range(2)]
        ff_bias_in = [sem(f"ff_bias_in{k}") for k in range(2)]

        add_w_in = sem("add_w_in")
        rep_ready = sem("rep_ready")
        text_psum = sem("text_psum")
        text_ready = sem("text_ready")
        feat_psum = sem("feat_psum")
        feat_ready = sem("feat_ready")
        tanh_ready = sem("tanh_ready")
        rho_psum = sem("rho_psum")
        rho_taken = sem("rho_taken")
        rho_stored = [sem(f"rho_stored{k}") for k in range(2)]
        rho_in = sem("rho_in")
        rhoT_psum = sem("rhoT_psum")
        rho_shifted = sem("rho_shifted")
        rho_exp = sem("rho_exp")
        gate_sums = sem("gate_sums")
        gate_tanh = sem("gate_tanh")
        moe_gate_in = sem("moe_gate_in")
        moe_gates_psum = sem("moe_gates_psum")
        moe_sigmoid = sem("moe_sigmoid")
        moe_gates_ready = sem("moe_gates_ready")
        moe_w_in = sem("moe_w_in")
        moe_oe_in = sem("moe_oe_in")
        qk_psum = sem("qk_psum")
        qk_ready = sem("qk_ready")
        v_psum = sem("v_psum")
        v_gated = sem("v_gated")
        v_ready = sem("v_ready")
        s_psum = sem("s_psum")
        s_max = sem("s_max")
        s_exp = sem("s_exp")
        pT_psum = sem("pT_psum")
        pT_ready = sem("pT_ready")
        o_psum = sem("o_psum")
        g_ready = sem("g_ready")
        gT_psum = sem("gT_psum")
        gT_ready = sem("gT_ready")
        y_psum = sem("y_psum")
        y_taken = sem("y_taken")
        dist_in = sem("dist_in")
        tb_in = sem("tb_in")
        ff_w_in = sem("ff_w_in")
        gn_var = sem("gn_var")
        gn_rstd = sem("gn_rstd")
        gn_ready = sem("gn_ready")
        gnT_psum = sem("gnT_psum")
        gnT_ready = sem("gnT_ready")
        hid_psum = sem("hid_psum")
        hid_ready = sem("hid_ready")
        down_psum = sem("down_psum")
        down_taken = sem("down_taken")
        sign_in = sem("sign_in")
        sign_ready = sem("sign_ready")
        sign_psum = sem("sign_psum")
        sign_taken = sem("sign_taken")
        bias_rep_ready = sem("bias_rep_ready")
        head_bias_in = sem("head_bias_in")

        block = ctx.enter_context(nc.Block())

        def end_phase(eng, which):
            eng.drain()
            eng.sem_inc(ends[which], 1)

        def begin_phase(eng, which, count):
            for other in ends:
                if other != which:
                    eng.wait_ge(ends[other], count)

        def probsT_base(n):
            return n * 48

        def ring_uses(t, s):
            return (t // 2 + 1) * 16 if isinstance(t, int) else (t - s + 2) * 8

        def rows_at(dram, t):
            return dram[t * P:(t + 1) * P, :] if isinstance(t, int) else dram[bass.ds(t * P, P), :]

        LN, DECODER = "ln", "decoder"


        def bias_rows(v, run):
            _, nb, nh = run
            return v.unsqueeze(1).unsqueeze(1).broadcast_to([P, nb, nh, KEYS])

        def logit_banks(cfg, run):
            b0, nb, nh = run
            return ps[:, b0:b0 + nb, 0:nh * KEYS].rearrange("p b (h k) -> p b h k", k=KEYS)

        def head_cols(v, cfg, run):
            b0, nb, nh = run
            h0 = b0 * cfg.hpb
            return v[:, h0 * KEYS:(h0 + nb * nh) * KEYS].rearrange(
                "p (b h k) -> p b h k", b=nb, k=KEYS)

        def head_scal(v, cfg, run, spread):
            b0, nb, nh = run
            h0 = b0 * cfg.hpb
            s = v[:, h0:h0 + nb * nh].rearrange("p (b h) -> p b h", b=nb)
            return s.unsqueeze(3).broadcast_to([P, nb, nh, KEYS]) if spread else s

        def fold_index(cfg):
            return [(c, b, h) for c in range(cfg.chunks) for b in range(B) for h in range(cfg.hpc)]

        KV_BASE = {"masked": 0, "timed": 4, "swish": 4 + 16 * LAYERS}
        FOLD_BASE = {"masked": 0, "timed": 48, "swish": 48 * (1 + LAYERS)}

        def plan(cfg, layer=0):
            n = {"masked": 0, "timed": 1, "swish": 1 + LAYERS}[cfg.kind] + layer
            kv = {"masked": 0, "timed": 4, "swish": 4 + 16 * LAYERS}[cfg.kind] + 16 * layer
            fold = {"masked": 0, "timed": 48, "swish": 48 * (1 + LAYERS)}[cfg.kind] + 48 * layer
            rings = {"masked": 0, "timed": 16, "swish": 16 * (1 + LAYERS)}[cfg.kind] + 16 * layer
            return n, kv, fold, rings

        @block.sync
        def _(sp):
            for name, dst in (("ident", ident), ("tri", tri), ("bd_mask", bd_mask),
                              ("earlier", earlier.rearrange("p a b -> p (a b)")), ("later8", later8),
                              ("ctxT", ctxT.rearrange("p a b -> p (a b)")), ("bo", cols_bo)):
                sp.dma_start(dst, a[name]).then_inc(consts_in, 16)
            sp.dma_start(x, a["x"].rearrange("p (t d) -> p t d", d=D)).then_inc(x_in, 16)
            sp.dma_start(mask_i, a["mask_keep"]).then_inc(mask_in, 16)

            def attention_weights(cfg, src, layer=None):
                for key, dst in (("wk", w_k), ("wv", w_v), ("wq", w_q), ("wo", w_o)):
                    if layer is None:
                        s = a[src + key]
                    elif isinstance(layer, int):
                        s = a[src + key][layer]
                    else:
                        s = a[src + key][bass.ds(layer, 1)].rearrange("a p k n -> (a p) k n")
                    if key in ("wk", "wv"):
                        d = dst[:, :, 0:cfg.width]
                    else:
                        d = dst[:, 0:cfg.chunks, :]
                    sp.dma_start(d, s).then_inc(att_w_in, 16)

            def fold_values_through_dram(cfg, layer=0):
                n, kv, fold, rings = plan(cfg, layer)
                sp.wait_ge(fold_ready, fold + cfg.b_units)
                for b in range(B):
                    sp.dma_start(scratch_b[b, 0:cfg.cols, :].rearrange("(h t) d -> t h d", t=KEYS),
                                 fold_v_rows[0:KEYS, b, 0:cfg.heads, :]).then_inc(fold_v_saved, 16)
                sp.wait_ge(fold_v_saved, n * 32 + 32)
                full = (cfg.rows - 1) * P
                for b in range(B):
                    sp.dma_start(fold_v[:, b, 0:cfg.rows - 1, :],
                                 scratch_b[b, 0:full, :].rearrange("(j p) d -> p j d", p=P)).then_inc(fold_v_in, 16)
                    sp.dma_start(fold_v[0:cfg.tail, b, cfg.rows - 1, :],
                                 scratch_b[b, full:cfg.cols, :]).then_inc(fold_v_in, 16)

            attention_weights(MASKED, "L0_")
            fold_values_through_dram(MASKED)

            def slots_of(run, sp=sp):
                def load(t, slot):
                    sp.wait_ge(ff_xT_psum, run.base + t - 1)
                    sp.dma_start(xn[:, slot, :], rows_at(slots_x[run.index], t)).then_inc(ff_x_in[slot], 16)
                    if run.kind == "gelu":
                        e = sp.value_load(tile_expert[0:1, t:t + 1] if isinstance(t, int) else
                                          tile_expert[0:1, bass.ds(t, 1)], min_val=0, max_val=7)
                        sp.wait_ge(ff_y_ready, run.base + t - 1)
                        sp.dma_start(ff_b1[:, slot, :], a["L3_b1"][bass.ds(e, 1), :].broadcast_to([P, HID])).then_inc(ff_bias_in[slot], 16)
                        sp.dma_start(ff_b2[:, slot, :], a["L3_b2"][bass.ds(e, 1), :].broadcast_to([P, D])).then_inc(ff_bias_in[slot], 16)

                def store(t, slot):
                    sp.wait_ge(ff_y_ready, run.base + t + 1)
                    sp.dma_start(rows_at(slots_y[run.index], t), ff_y[:, slot, :]).then_inc(ff_y_stored[slot], 16)

                load(0, 0)
                load(1, 1)
                with sp.Fori(0, run.tiles // 2 - 1) as i:
                    for s in range(2):
                        load(i * 2 + s + 2, s)
                        store(i * 2 + s, s)
                store(run.tiles - 2, 0)
                store(run.tiles - 1, 1)

            if STOP_AFTER >= 2:
                sp.wait_ge(zeros_made, 1)
                for n, run in enumerate((SWIGLU, GELU)):
                    sp.dma_start(slots_x[n].rearrange("(j p) d -> p j d", p=P),
                                 zero_row.unsqueeze(1).broadcast_to([P, run.tiles, D])).then_inc(zeroed, 16)
                for other in ("pe", "act", "dve", "pool"):
                    sp.wait_ge(ends[other], 1)
                sp.dma_start(before, a["before"]).then_inc(route_consts_in, 16)
                sp.dma_start(ones, a["ones"]).then_inc(route_consts_in, 16)
                sp.dma_start(tile_of, a["tile_of"]).then_inc(route_consts_in, 16)
                sp.dma_start(w_router, a["L0_gate"]).then_inc(route_consts_in, 16)
                order = (8, 0, 1, 2, 3, 4, 5, 6, 7)
                for e in order:
                    sp.dma_start(w13[:, e, :, :], a["L0_w13"][e]).then_inc(expert_landed[e], 16)
                    sp.dma_start(w2e[:, e, :, :], a["L0_w2"][e]).then_inc(expert_landed[e], 16)
                for e in order:
                    sp.wait_ge(expert_landed[e], 32)
                    sp.sem_inc(experts_in, 1)
                for c in range(2):
                    sp.wait_ge(row_scattered[c], TILES * 16)
                slots_of(SWIGLU)

            def phase_over(count):
                for other in ends:
                    sp.wait_ge(ends[other], count)

            if STOP_AFTER >= 3:
                phase_over(2)
                for name, dst in (("L1_Ws", w_text), ("L1_W", w_feat)):
                    sp.dma_start(dst, a[name]).then_inc(add_w_in, 16)
                for name, dst in (("L1_cols", gate_cols), ("L1_b", add_bias), ("L1_sb", scal_bias),
                                  ("q_mask", q_mask_i)):
                    sp.dma_start(dst, a[name]).then_inc(add_w_in, 16)

                def store_scores(t, slot):
                    sp.wait_ge(rho_taken, t + 1)
                    row = scores_dram[t:t + 1, :] if isinstance(t, int) else scores_dram[bass.ds(t, 1), :]
                    sp.dma_start(row.rearrange("a (q n) -> (a q) n", q=4),
                                 score_rows[0:P:32, slot, :]).then_inc(rho_stored[slot], 16)

                with sp.Fori(0, KEYS // 2) as i:
                    store_scores(i * 2, 0)
                    store_scores(i * 2 + 1, 1)
                store_scores(KEYS - 1, 0)
                sp.wait_ge(rho_stored[0], (KEYS // 2 + 1) * 16)
                sp.wait_ge(rho_stored[1], KEYS // 2 * 16)
                sp.dma_start(rho_rows, scores_dram.rearrange("k (b n) -> k b n", b=B)).then_inc(rho_in, 16)
            if STOP_AFTER >= 4:
                phase_over(3)
                sp.dma_start(dist, a["dist"]).then_inc(dist_in, 16)
                sp.dma_start(ff0, a["ff0"]).then_inc(dist_in, 16)
                sp.dma_start(tb, a["tb"][0]).then_inc(tb_in, 16)
                sp.dma_start(w_gate, a["L1_gate"]).then_inc(moe_gate_in, 16)

                def pair_weights(hp):
                    one = (lambda v: v[hp]) if isinstance(hp, int) else (
                        lambda v: v[bass.ds(hp, 1)].rearrange("a p n -> (a p) n"))
                    sp.dma_start(w_qk.rearrange("p a b n -> p (a b n)"), one(a["L1_wqk"])).then_inc(moe_w_in, 16)
                    sp.dma_start(w_ve.rearrange("p a b n -> p (a b n)"), one(a["L1_ve"])).then_inc(moe_w_in, 16)

                def pair_outputs(hp):
                    one = (lambda v: v[hp]) if isinstance(hp, int) else (
                        lambda v: v[bass.ds(hp, 1)].rearrange("a p n -> (a p) n"))
                    sp.dma_start(w_oe.rearrange("p a b n -> p (a b n)"), one(a["L1_oe"])).then_inc(moe_oe_in, 16)

                pair_weights(0)
                pair_outputs(0)
                with sp.Fori(1, 4) as hp:
                    sp.wait_ge(v_psum, hp * 32)
                    pair_weights(hp)
                    sp.wait_ge(y_psum, hp * 16)
                    pair_outputs(hp)
            if STOP_AFTER >= 5:
                phase_over(4)
                attention_weights(TIMED, "L2_", 0)

                def layer(l, last=False):
                    row = (lambda v, k=None: v[l]) if isinstance(l, int) else (
                        lambda v: v[bass.ds(l, 1)].rearrange("a p n -> (a p) n"))
                    phase_over(l * 2 + 4)
                    sp.dma_start(w_f1.rearrange("p a n -> p (a n)"), row(a["L2_f1"])).then_inc(ff_w_in, 16)
                    sp.dma_start(w_f2.rearrange("p a n -> p (a n)"), row(a["L2_f2"])).then_inc(ff_w_in, 16)
                    sp.dma_start(b_f1, row(a["L2_bf1"])).then_inc(ff_w_in, 16)
                    sp.dma_start(b_f2, row(a["L2_bf2"])).then_inc(ff_w_in, 16)
                    if not last:
                        sp.wait_ge(relu_used, l * 32 + 34)
                        sp.dma_start(tb, a["tb"][bass.ds(l + 1, 1)].rearrange("a p n -> (a p) n")).then_inc(tb_in, 16)
                    fold_values_through_dram(TIMED, l)
                    if not last:
                        sp.wait_ge(fold_psum, plan(TIMED, l)[2] + 48)
                        attention_weights(TIMED, "L2_", l + 1)

                with sp.Fori(0, LAYERS - 1) as l:
                    layer(l)
                layer(LAYERS - 1, last=True)
            if STOP_AFTER >= 6:
                phase_over(13)
                sp.dma_start(w_raw, a["L2_sign"]).then_inc(sign_in, 16)
            if STOP_AFTER >= 7:
                phase_over(14)
                sp.dma_start(head_bias, a["L3_qb"]).then_inc(head_bias_in, 16)
                attention_weights(SWISH, "L3_")
                fold_values_through_dram(SWISH)
            if STOP_AFTER >= 8:
                phase_over(15)
                sp.dma_start(before, a["before"]).then_inc(route_consts_in, 16)
                sp.dma_start(ones, a["ones"]).then_inc(route_consts_in, 16)
                sp.dma_start(tile_of, a["tile_of"]).then_inc(route_consts_in, 16)
                sp.dma_start(w_redT, a["L3_redT"]).then_inc(route_consts_in, 16)
                sp.dma_start(wg, a["L3_wg"]).then_inc(route_consts_in, 16)
                for e in range(EXPERTS):
                    sp.dma_start(w1g[:, e, :, :], a["L3_w1"][e]).then_inc(gelu_landed[e], 16)
                    sp.dma_start(w2g[:, e, :, :], a["L3_w2"][e]).then_inc(gelu_landed[e], 16)
                sp.wait_ge(row_scattered[0], 2 * TILES * 16)
                slots_of(GELU)

            sp.wait_ge(end_dve, (0, 1, 2, 3, 4, 13, 14, 15, 16)[min(STOP_AFTER, 8)])
            sp.dma_start(out.rearrange("p (t d) -> p t d", d=D), x).then_inc(out_stored, 16)
            sp.wait_ge(out_stored, 16)

        @block.tensor
        def _(pe):
            mm = nc.tensor.matmul

            def context_attention(cfg, ring, layer=0):
                n, kv, fold, att = plan(cfg, layer)
                pe.wait_ge(att_w_in, (n + 1) * 64)

                def head_rows(c, w):
                    for k in range(KC):
                        last = mm(ps[:, c % 2, 0:B * KEYS], w[:, k, c * P:(c + 1) * P], ctxT[:, k, :],
                                  start=(k == 0), stop=(k == KC - 1))
                    last.then_inc(bd_psum, 1)

                unit = 0

                def bank():
                    if unit >= 6:
                        pe.wait_ge(fold_ready, fold + unit - 5)
                    return 2 + unit % 6

                head_rows(0, w_v)
                for c in range(cfg.chunks):
                    if c + 1 < cfg.chunks:
                        head_rows(c + 1, w_v)
                    pe.wait_ge(bd_ready, kv + c + 1)
                    bd = view(bd_off + (c % 2) * B * 616, B, cfg.hpc * KEYS)
                    for b in range(B):
                        for h in range(cfg.hpc):
                            mm(ps[0:KEYS, bank(), 0:D], bd[:, b, h * KEYS:(h + 1) * KEYS], w_o[:, c, :],
                               start=True, stop=True).then_inc(fold_psum, 1)
                            unit += 1
                for c in range(cfg.chunks + 1):
                    if c < cfg.chunks:
                        cc = c + cfg.chunks
                        for k in range(KC):
                            last = mm(ps[:, cc % 2, 0:B * KEYS], w_k[:, k, c * P:(c + 1) * P], ctxT[:, k, :],
                                      start=(k == 0), stop=(k == KC - 1))
                        last.then_inc(bd_psum, 1)
                    if c == 0:
                        continue
                    g = c - 1
                    cc = g + cfg.chunks
                    pe.wait_ge(bd_ready, kv + cc + 1)
                    bd = view(bd_off + (cc % 2) * B * 616, B * cfg.hpc * KEYS)
                    for u in range(cfg.halves):
                        for m in range(KC):
                            mm(ps[:, bank(), 0:308], w_q[:, g, m * P:(m + 1) * P],
                               bd[:, u * 308:(u + 1) * 308], start=True, stop=True).then_inc(fold_psum, 1)
                            unit += 1
                        if cfg.kind == "swish":
                            pe.wait_ge(bias_rep_ready, 1)
                            mm(ps[:, bank(), 0:308], head_bias_rep[:, g, :], bd[:, 0:308],
                               start=True, stop=True).then_inc(fold_psum, 1)
                            unit += 1
                pe.wait_ge(fold_ready, fold + unit)

                def transpose_tile(t, slot):
                    pe.wait_ge(xn_ready, ring + t + 1)
                    if not (isinstance(t, int) and t == 0):
                        pe.wait_ge(xnT_ready, ring + t)
                    for k in range(KC):
                        last = nc.tensor.transpose(ps[:, 3, k * P:(k + 1) * P],
                                                   xn[:, slot, k * P:(k + 1) * P], ident)
                    last.then_inc(xnT_psum, 1)

                def logits(t, slot):
                    pe.wait_ge(xnT_ready, ring + t + 1)
                    if not (isinstance(t, int) and t == 0):
                        pe.wait_ge(shifted_ready, att + t)
                    nb = -(-cfg.heads // cfg.hpb)
                    for bk in range(nb):
                        h0 = bk * cfg.hpb
                        w = min(cfg.hpb, cfg.heads - h0) * KEYS
                        for k in range(KC):
                            last = mm(ps[:, bk, 0:w], xnT[:, slot, k, :],
                                      fold_q[:, k, slot, h0 * KEYS:h0 * KEYS + w],
                                      start=(k == 0), stop=(k == KC - 1))
                    last.then_inc(logits_ready, 1)

                def weighted_values(t, slot, first=False):
                    pe.wait_ge(probs_ready, att + t + 1)
                    for j in range(cfg.rows):
                        r = P if j < cfg.rows - 1 else cfg.tail
                        last = nc.tensor.transpose(ps[0:r, 4 + j // 4, (j % 4) * P:(j % 4 + 1) * P],
                                                   probs[:, slot, j * P:j * P + r], ident)
                        if j % 4 == 3 or j == cfg.rows - 1:
                            last.then_inc(probsT_psum, 1)
                    if first:
                        pe.wait_ge(fold_v_in, (n + 1) * 64)
                    if not first:
                        pe.wait_ge(x_updated, att + t)
                    parts = -(-cfg.rows // 4)
                    for j in range(cfg.rows):
                        r = P if j < cfg.rows - 1 else cfg.tail
                        if j % 4 == 0:
                            pe.wait_ge(probsT_ready, probsT_base(n) + t * parts + j // 4 + 1)
                        last = mm(ps[:, 7, 0:D], probsT[0:r, slot, j, :],
                                  fold_v[0:r, slot, j, :], start=(j == 0), stop=(j == cfg.rows - 1))
                    last.then_inc(att_out, 1)

                transpose_tile(0, 0)
                transpose_tile(1, 1)
                logits(0, 0)

                def step(t, s, **kw):
                    transpose_tile(t + 1, 1 - s)
                    logits(t, s)
                    weighted_values(t - 1, 1 - s, **kw)

                step(1, 1, first=True)
                step(2, 0)
                with pe.Fori(0, 6) as i:
                    step(i * 2 + 3, 1)
                    step(i * 2 + 4, 0)
                logits(15, 1)
                weighted_values(14, 0)
                weighted_values(15, 1)

            pe.wait_ge(consts_in, 112)
            context_attention(MASKED, 0)
            end_phase(pe, "pe")

            def transpose_all(n, a0, after):
                for pair in range(TILES // 2):
                    u = n * 8 + pair
                    pe.wait_ge(all_xn_ready, a0 * 16 + 2 * pair + 2)
                    if pair >= 2:
                        pe.wait_ge(rt_ready, u - 1)
                    for t2 in range(2):
                        for k in range(KC):
                            c = (k * 2 + t2) * P
                            last = nc.tensor.transpose(ps[:, 6 + pair % 2, c:c + P],
                                                       z[:, 2 * pair + t2, k * P:(k + 1) * P], ident)
                    last.then_inc(rt_psum, 1)
                    if pair >= 1:
                        after(pair - 1, u)
                after(TILES // 2 - 1, n * 8 + 8)

            def router(n):
                def scores(pair, ready):
                    pe.wait_ge(rt_ready, ready)
                    for t2 in range(2):
                        t = 2 * pair + t2
                        for k in range(KC):
                            last = mm(ps[:, 5, t * 8:t * 8 + 8], pairT[:, pair % 2, k, t2 * P:(t2 + 1) * P],
                                      w_router[:, k, :], start=(k == 0), stop=(k == KC - 1))
                    if pair == TILES // 2 - 1:
                        last.then_inc(router_ready, 1)
                return scores

            def ranks(r):
                pe.wait_ge(chosen_ready, r + 1)
                chosen = route[2].rearrange("p t e -> p (t e)")
                mm(ps[:, 3, 0:P], before, chosen, start=True, stop=True)
                mm(ps[:, 4, 0:P], ones, chosen, start=True, stop=True).then_inc(ranks_ready, 1)

            def expert_tiles(run):
                b = run.base
                ff_h = ff_h_gelu if run.kind == "gelu" else ff_h_swiglu

                def transposed(t, slot, fresh=False):
                    if run.kind == "shared":
                        pe.wait_ge(ff_x_handed, t + 1)
                    else:
                        pe.wait_ge(ff_x_in[slot], ring_uses(t, slot) + run.loaded * 8)
                    if not fresh:
                        pe.wait_ge(ff_xT_ready, b + t)
                    for k in range(KC):
                        last = nc.tensor.transpose(ps[:, 0, k * P:(k + 1) * P], xn[:, slot, k * P:(k + 1) * P], ident)
                    last.then_inc(ff_xT_psum, 1)

                def up(t, slot):
                    pe.wait_ge(ff_xT_ready, b + t + 1)
                    if not (isinstance(t, int) and t == 0):
                        pe.wait_ge(ff_biased if run.kind == "gelu" else ff_h_ready, (0 if run.kind == "gelu" else b) + t)
                    if run.kind == "shared":
                        pe.wait_ge(experts_in, 1)
                        e = 8
                    else:
                        e = pe.value_load(tile_expert[0:1, t:t + 1] if isinstance(t, int) else
                                          tile_expert[0:1, bass.ds(t, 1)], min_val=0, max_val=7)
                        pe.wait_ge(experts_in, e + (2 if run.kind == "swiglu" else 10))
                    for half in range(run.up // 512):
                        for k in range(KC):
                            if run.kind == "shared":
                                w = w13[:, 8, k, :]
                            elif run.kind == "swiglu":
                                w = w13[:, bass.ds(e, 1), k, :].rearrange("p a n -> p (a n)")
                            else:
                                w = w1g[:, bass.ds(e, 1), k, half * 512:(half + 1) * 512].rearrange("p a n -> p (a n)")
                            last = mm(ps[:, 1 + half, :], xnT[:, slot, k, :], w, start=(k == 0), stop=(k == KC - 1))
                    last.then_inc(ff_up, 1)
                    return e

                def hidden(t, slot):
                    pe.wait_ge(ff_h_ready, b + t + 1)
                    for c in range(run.chunks):
                        last = nc.tensor.transpose(ps[:, 3 + c // 4, (c % 4) * P:(c % 4 + 1) * P],
                                                   ff_h[:, slot, c * P:(c + 1) * P], ident)
                        if c % 4 == 3 or c == run.chunks - 1:
                            last.then_inc(ff_hT_psum, 1)

                def down(t, slot, fresh=False):
                    parts = -(-run.chunks // 4)
                    hb = run.base if run.kind != "gelu" else 56
                    if run.kind == "shared":
                        e = 8
                    else:
                        e = pe.value_load(tile_expert[0:1, t:t + 1] if isinstance(t, int) else
                                          tile_expert[0:1, bass.ds(t, 1)], min_val=0, max_val=7)
                    if not fresh:
                        pe.wait_ge(ff_y_ready, b + t)
                    for c in range(run.chunks):
                        if c % 4 == 0:
                            pe.wait_ge(ff_hT_ready, hb + t * parts + c // 4 + 1)
                        if run.kind == "shared":
                            w = w2e[:, 8, c, :]
                        elif run.kind == "swiglu":
                            w = w2e[:, bass.ds(e, 1), c, :].rearrange("p a n -> p (a n)")
                        else:
                            w = w2g[:, bass.ds(e, 1), c, :].rearrange("p a n -> p (a n)")
                        last = mm(ps[:, 5, 0:D], ff_hT[:, slot, c * P:(c + 1) * P], w,
                                  start=(c == 0), stop=(c == run.chunks - 1))
                    last.then_inc(ff_y_psum, 1)

                transposed(0, 0, fresh=(b == 0))
                up(0, 0)
                transposed(1, 1)
                hidden(0, 0)
                up(1, 1)
                down(0, 0, fresh=(b == 0))

                def step(t, s):
                    transposed(t, s)
                    hidden(t - 1, 1 - s)
                    up(t, s)
                    down(t - 1, 1 - s)

                with pe.Fori(0, run.tiles // 2 - 1) as i:
                    step(i * 2 + 2, 0)
                    step(i * 2 + 3, 1)
                hidden(run.tiles - 1, 1)
                down(run.tiles - 1, 1)

            if STOP_AFTER >= 2:
                pe.wait_ge(route_consts_in, 64)
                transpose_all(0, 0, router(0))
                ranks(0)
                expert_tiles(SHARED)
                expert_tiles(SWIGLU)
                end_phase(pe, "pe")

            if STOP_AFTER >= 3:
                begin_phase(pe, "pe", 2)
                pe.wait_ge(rep_ready, 1)
                for m in range(KC):
                    for k in range(KC):
                        mm(ps[:, 4, m * 154:(m + 1) * 154], w_text[:, k, m * P:(m + 1) * P], ctxT[:, k, :],
                           start=(k == 0), stop=(k == KC - 1))
                for w in range(2):
                    for k in range(KC):
                        last = mm(ps[:, 5, w * 154:(w + 1) * 154], gate_rep[:, w, k, :], ctxT[:, k, :],
                                  start=(k == 0), stop=(k == KC - 1))
                last.then_inc(text_psum, 1)

                def features(pair, ready):
                    pe.wait_ge(rt_ready, ready)
                    if pair >= 2:
                        pe.wait_ge(feat_ready, pair - 1)
                    for m in range(KC):
                        for k in range(KC):
                            last = mm(ps[:, 2 * (pair % 2) + m, 0:256], w_feat[:, k, m * P:(m + 1) * P],
                                      pairT2[:, pair % 2, k, :], start=(k == 0), stop=(k == KC - 1))
                    last.then_inc(feat_psum, 1)

                transpose_all(1, 1, features)
                pe.wait_ge(feat_ready, TILES // 2)
                def text_scores(t, slot, fresh=False):
                    pe.wait_ge(tanh_ready, t + 1)
                    if not fresh:
                        pe.wait_ge(rho_taken, t - 1)
                    for m in range(KC):
                        for q in range(4):
                            b, half = divmod(q, 2)
                            last = mm(ps[32 * q:32 * q + 32, slot, :], w_col[:, m, :],
                                      tanhT[:, slot, b, m, half * GT:(half + 1) * GT],
                                      start=(m == 0), stop=(m == KC - 1), tile_position=(0, 32 * q))
                    last.then_inc(rho_psum, 1)

                text_scores(0, 0, fresh=True)
                text_scores(1, 1, fresh=True)
                with pe.Fori(0, KEYS // 2 - 1) as i:
                    text_scores(i * 2 + 2, 0)
                    text_scores(i * 2 + 3, 1)
                text_scores(KEYS - 1, 0)
                pe.wait_ge(rho_in, 16)
                pe.wait_ge(rho_taken, KEYS)
                for b in range(B):
                    for j in range(TILES // 2):
                        u = 8 * b + j
                        last = nc.tensor.transpose(ps[:, 2 + u // 6, (u % 6) * KEYS:(u % 6 + 1) * KEYS],
                                                   rho_rows[:, b, j * P:(j + 1) * P], ident[0:KEYS, 0:KEYS])
                last.then_inc(rhoT_psum, 1)
                end_phase(pe, "pe")

            if STOP_AFTER >= 4:
                begin_phase(pe, "pe", 3)
                pe.wait_ge(moe_gate_in, 16)

                def gate_scores(pair, ready):
                    pe.wait_ge(rt_ready, ready)
                    for t2 in range(2):
                        t = 2 * pair + t2
                        for k in range(KC):
                            last = mm(ps[:, 4 + t // 8, (t % 8) * 64:(t % 8 + 1) * 64], xnT_all[:, k, t * P:(t + 1) * P],
                                      w_gate[:, k, :], start=(k == 0), stop=(k == KC - 1))
                    if pair == TILES // 2 - 1:
                        last.then_inc(moe_gates_psum, 1)

                transpose_all(2, 2, gate_scores)
                pe.wait_ge(moe_gates_ready, 1)
                units = [(b, i, h) for b in range(B) for i in range(TILES // 2) for h in range(2)]
                with pe.Fori(0, 4) as hp:
                    pe.wait_ge(moe_w_in, hp * 32 + 32)
                    for u in range(8):
                        q, which = divmod(u, 2)
                        if u >= 4:
                            pe.wait_ge(qk_ready, hp * 8 + (u - 3))
                        for k in range(KC):
                            last = mm(ps[:, u % 4, :], w_qk[:, k, which, :], xnT_all[:, k, q * GT:(q + 1) * GT],
                                      start=(k == 0), stop=(k == KC - 1))
                        last.then_inc(qk_psum, 1)
                    pe.wait_ge(y_taken, hp * 16 + 1)
                    for w in range(32):
                        t, h = divmod(w, 2)
                        if w >= 4:
                            pe.wait_ge(v_gated, hp * 32 + (w - 3))
                        for k in range(KC):
                            last = mm(ps[:, 4 + w % 4, :], xnT_all[:, k, t * P:(t + 1) * P], w_ve[:, k, h, :],
                                      start=(k == 0), stop=(k == KC - 1))
                        last.then_inc(v_psum, 1)
                    pe.wait_ge(qk_ready, hp * 8 + 8)
                    pe.wait_ge(v_ready, hp * 32 + 32)

                    def scores(u):
                        b, i, h = units[u]
                        if u >= 1:
                            pe.wait_ge(s_exp, hp * 32 + u)
                        r = slice(64 * h, 64 * h + 64)
                        for half in range(1 + i // 4):
                            n = min((i + 1) * P - half * GT, GT)
                            last = mm(ps[:, half, 0:n], QT[r, b, i * P:(i + 1) * P], KT[r, b, half * GT:half * GT + n],
                                      start=True, stop=True)
                        last.then_inc(s_psum, 1)

                    def mixT(u):
                        b, i, h = units[u]
                        pe.wait_ge(s_exp, hp * 32 + u + 1)
                        for j in range(i + 1):
                            last = nc.tensor.transpose(ps[:, 2 + j // 4, (j % 4) * P:(j % 4 + 1) * P],
                                                       P_sb[:, u % 2, j * P:(j + 1) * P], ident)
                        last.then_inc(pT_psum, 1)

                    def mixed(u):
                        b, i, h = units[u]
                        if u >= 1:
                            pe.wait_ge(g_ready, hp * 32 + u)
                        pe.wait_ge(pT_ready, hp * 32 + u + 1)
                        for j in range(i + 1):
                            last = mm(ps[:, 4, 0:P], PT_sb[:, u % 2, j, :], V[:, 2 * j + b, :, :].rearrange("p h k -> p (h k)"),
                                      start=(j == 0), stop=(j == i))
                        last.then_inc(o_psum, 1)

                    def gatedT(u):
                        pe.wait_ge(g_ready, hp * 32 + u + 1)
                        for c in range(4):
                            last = nc.tensor.transpose(ps[:, 5, c * P:(c + 1) * P], G_sb[:, u % 2, c * P:(c + 1) * P], ident)
                        last.then_inc(gT_psum, 1)

                    def gated(u):
                        b, i, h = units[u]
                        if u == 0:
                            pe.wait_ge(moe_oe_in, hp * 16 + 16)
                        if h == 0 and u >= 4:
                            pe.wait_ge(y_taken, hp * 16 + (u // 2))
                        pe.wait_ge(gT_ready, hp * 32 + u + 1)
                        for c in range(4):
                            last = mm(ps[:, 6 + (u // 2) % 2, 0:D], GT_sb[:, u % 2, c, :], w_oe[:, h, c, :],
                                      start=(h == 0 and c == 0), stop=(h == 1 and c == 3))
                        if h == 1:
                            last.then_inc(y_psum, 1)

                    for u in range(len(units) + 2):
                        if 1 <= u <= len(units):
                            mixT(u - 1)
                        if u >= 2:
                            gatedT(u - 2)
                        if u < len(units):
                            scores(u)
                        if 1 <= u <= len(units):
                            mixed(u - 1)
                        if u >= 2:
                            gated(u - 2)
                end_phase(pe, "pe")

            if STOP_AFTER >= 5:
                with pe.Fori(0, LAYERS) as l:
                    begin_phase(pe, "pe", l * 2 + 4)
                    context_attention(TIMED, l * 16 + 16, l)
                    end_phase(pe, "pe")
                    begin_phase(pe, "pe", l * 2 + 5)
                    pe.wait_ge(ff_w_in, l * 64 + 64)

                    def transposed(q):
                        pe.wait_ge(gn_ready, l * 4 + (q + 1))
                        for t in range(4):
                            for k in range(KC):
                                c = (t % 2) * P + k * 2 * P
                                last = nc.tensor.transpose(ps[:, 4 + t // 2, c:c + P], xng[:, t, k * P:(k + 1) * P], ident)
                        last.then_inc(gnT_psum, 1)

                    def up(q):
                        pe.wait_ge(gnT_ready, l * 4 + (q + 1))
                        for m in range(8):
                            if q >= 1 or m >= 4:
                                pe.wait_ge(hid_ready, l * 32 + (q * 8 + m - 3))
                            for k in range(KC):
                                last = mm(ps[:, m % 4, :], w_f1[:, k, m * P:(m + 1) * P], gT[:, q % 2, k, :],
                                          start=(k == 0), stop=(k == KC - 1))
                            last.then_inc(hid_psum, 1)

                    def down(q):
                        for t in range(4):
                            if t % 2 == 0 and q >= 1:
                                pe.wait_ge(down_taken, l * 8 + (2 * q + t // 2 - 1))
                            for m in range(8):
                                if t == 0:
                                    pe.wait_ge(hid_ready, l * 32 + (q * 8 + m + 1))
                                last = mm(ps[:, 6 + t // 2, (t % 2) * D:(t % 2 + 1) * D], hidT[:, m, t * P:(t + 1) * P],
                                          w_f2[:, m, :], start=(m == 0), stop=(m == 7))
                            if t % 2 == 1:
                                last.then_inc(down_psum, 1)

                    transposed(0)
                    for q in range(GROUPS):
                        up(q)
                        if q + 1 < GROUPS:
                            transposed(q + 1)
                        down(q)
                    end_phase(pe, "pe")
                end_phase(pe, "pe")

            if STOP_AFTER >= 6:
                begin_phase(pe, "pe", 13)
                pe.wait_ge(sign_ready, 1)

                def project(pair, ready):
                    pe.wait_ge(rt_ready, ready)
                    if pair >= 2:
                        pe.wait_ge(sign_taken, pair - 1)
                    for t2 in range(2):
                        for k in range(KC):
                            last = mm(ps[:, pair % 2, t2 * D:(t2 + 1) * D], pairT3[:, pair % 2, k, t2 * P:(t2 + 1) * P],
                                      w_sign[:, k, :], start=(k == 0), stop=(k == KC - 1))
                    last.then_inc(sign_psum, 1)

                transpose_all(3, 4, project)
                end_phase(pe, "pe")

            if STOP_AFTER >= 7:
                begin_phase(pe, "pe", 14)
                context_attention(SWISH, 80)
                end_phase(pe, "pe")

            if STOP_AFTER >= 8:
                begin_phase(pe, "pe", 15)
                pe.wait_ge(wg_ready, 1)
                nc.tensor.transpose(ps[0:16, 2, 0:8], wg, ident[0:8, 0:8]).then_inc(wgT_psum, 1)
                pe.wait_ge(wgT_ready, 1)
                for k in range(KC):
                    last = mm(ps[:, 2, 16 + 8 * k:24 + 8 * k], w_redT[:, k * P:(k + 1) * P], wgT, start=True, stop=True)
                last.then_inc(w_router_psum, 1)
                pe.wait_ge(w_router_ready, 1)
                transpose_all(4, 5, router(1))
                ranks(1)
                expert_tiles(GELU)
                end_phase(pe, "pe")

        @block.scalar
        def _(act):
            cp = nc.scalar.copy

            def context_attention(cfg, ring, layer=0):
                n, kv, fold, att = plan(cfg, layer)
                unit = 0
                for c, b, h in fold_index(cfg):
                    act.wait_ge(fold_psum, fold + unit + 1)
                    cp(fold_v_rows[0:KEYS, b, c * cfg.hpc + h, :], ps[0:KEYS, 2 + unit % 6, 0:D]).then_inc(fold_ready, 1)
                    unit += 1
                for c in range(cfg.chunks):
                    for u in range(cfg.halves):
                        for m in range(KC):
                            act.wait_ge(fold_psum, fold + unit + 1)
                            src = ps[:, 2 + unit % 6, 0:308]
                            if cfg.hpc * KEYS * B == 308:
                                dst = fold_q[:, m, :, c * 154:(c + 1) * 154]
                                src = src.rearrange("p (b k) -> p b k", b=B)
                            else:
                                b, half = divmod(u, cfg.halves // B)
                                o = c * cfg.hpc * KEYS + half * 308
                                dst = fold_q[:, m, b, o:o + 308]
                            nc.scalar.mul(dst, src, cfg.scale).then_inc(fold_ready, 1)
                            unit += 1
                        if cfg.kind == "swish":
                            act.wait_ge(fold_psum, fold + unit + 1)
                            cp(cbias[:, :, c * 154:(c + 1) * 154],
                               ps[:, 2 + unit % 6, 0:308].rearrange("p (b k) -> p b k", b=B)).then_inc(fold_ready, 1)
                            unit += 1

                def take_transpose(t, slot):
                    act.wait_ge(xnT_psum, ring + t + 1)
                    cp(xnT[:, slot, :, :], ps[:, 3, 0:D].rearrange(
                        "p (k n) -> p k n", k=KC)).then_inc(xnT_ready, 1)

                def take_probsT(t, slot):
                    parts = -(-cfg.rows // 4)
                    for q in range(parts):
                        act.wait_ge(probsT_psum, probsT_base(n) + t * parts + q + 1)
                        j1 = min(4 * q + 4, cfg.rows)
                        if j1 < cfg.rows or cfg.tail == P:
                            cp(probsT[:, slot, 4 * q:j1, :], ps[:, 4 + q, 0:(j1 - 4 * q) * P].rearrange(
                                "p (j n) -> p j n", n=P)).then_inc(probsT_ready, 1)
                        else:
                            if j1 - 1 > 4 * q:
                                cp(probsT[:, slot, 4 * q:j1 - 1, :], ps[:, 4 + q, 0:(j1 - 1 - 4 * q) * P].rearrange(
                                    "p (j n) -> p j n", n=P))
                            cp(probsT[0:cfg.tail, slot, j1 - 1, :],
                               ps[0:cfg.tail, 4 + q, (j1 - 1 - 4 * q) * P:(j1 - 4 * q) * P]).then_inc(probsT_ready, 1)

                def exponentials(t, slot):
                    act.wait_ge(shifted_ready, att + t + 1)
                    nc.scalar.activation(probs[:, slot, 0:cfg.cols], shifted[:, slot, 0:cfg.cols],
                                         ACT.Exp).then_inc(exp_ready, 1)

                take_transpose(0, 0)
                take_transpose(1, 1)
                act.wait_ge(fold_v_saved, n * 32 + 32)
                exponentials(0, 0)

                def step(t, s):
                    take_transpose(t + 1, 1 - s)
                    take_probsT(t - 1, 1 - s)
                    exponentials(t, s)

                step(1, 1)
                step(2, 0)
                with act.Fori(0, 6) as i:
                    step(i * 2 + 3, 1)
                    step(i * 2 + 4, 0)
                take_probsT(14, 0)
                exponentials(15, 1)
                take_probsT(15, 1)

            context_attention(MASKED, 0)
            end_phase(act, "act")

            def take_transposes(n, ring=None):
                for pair in range(TILES // 2):
                    act.wait_ge(rt_psum, n * 8 + pair + 1)
                    cp(xnT_all[:, :, pair * 256:(pair + 1) * 256] if ring is None else ring[:, pair % 2, :, :],
                       ps[:, 6 + pair % 2, :].rearrange("p (k n) -> p k n", k=KC)).then_inc(rt_ready, 1)

            def router_exponentials(r):
                act.wait_ge(router_shifted, r + 1)
                nc.scalar.activation(route[1], route[0], ACT.Exp).then_inc(router_exp, 1)

            def expert_tiles(run):
                b = run.base
                ff_h = ff_h_gelu if run.kind == "gelu" else ff_h_swiglu

                def transposed(t, slot):
                    act.wait_ge(ff_xT_psum, b + t + 1)
                    cp(xnT[:, slot, :, :], ps[:, 0, 0:D].rearrange("p (k n) -> p k n", k=KC)).then_inc(ff_xT_ready, 1)

                def function(t, slot):
                    if run.kind == "gelu":
                        act.wait_ge(ff_biased, t + 1)
                        nc.scalar.activation(ff_h[:, slot, :], ff_h[:, slot, :], ACT.Gelu).then_inc(ff_h_ready, 1)
                    else:
                        act.wait_ge(ff_up, b + t + 1)
                        nc.scalar.activation(ff_h[:, slot, 512:768], ps[:, 1, 0:256], ACT.Silu).then_inc(ff_gate, 1)

                def hidden(t, slot):
                    parts = -(-run.chunks // 4)
                    for q in range(parts):
                        act.wait_ge(ff_hT_psum, (run.base if run.kind != "gelu" else 56) + t * parts + q + 1)
                        w = min(4, run.chunks) * P
                        cp(ff_hT[:, slot, q * 512:q * 512 + w], ps[:, 3 + q, 0:w]).then_inc(ff_hT_ready, 1)

                transposed(0, 0)
                function(0, 0)
                transposed(1, 1)
                hidden(0, 0)
                function(1, 1)
                with act.Fori(0, run.tiles // 2 - 1) as i:
                    for s in range(2):
                        transposed(i * 2 + s + 2, s)
                        hidden(i * 2 + s + 1, 1 - s)
                        function(i * 2 + s + 2, s)
                hidden(run.tiles - 1, 1)

            if STOP_AFTER >= 2:
                take_transposes(0, pairT)
                router_exponentials(0)
                expert_tiles(SHARED)
                expert_tiles(SWIGLU)
                end_phase(act, "act")

            if STOP_AFTER >= 3:
                begin_phase(act, "act", 2)
                take_transposes(1, pairT2)
                act.wait_ge(text_ready, 1)
                act.wait_ge(feat_ready, TILES // 2)

                def tanhs(t, slot, fresh=False):
                    if not fresh:
                        act.wait_ge(rho_psum, t - 1)
                    for b in range(B):
                        for m in range(KC):
                            c = t + b * KEYS
                            bias = textT[:, m, c:c + 1] if isinstance(t, int) else textT[:, m, bass.ds(c, 1)]
                            last = nc.scalar.activation(tanhT[:, slot, b, m, :], featT[:, m, b, :], ACT.Tanh, bias=bias)
                    last.then_inc(tanh_ready, 1)

                tanhs(0, 0, fresh=True)
                tanhs(1, 1, fresh=True)
                with act.Fori(0, KEYS // 2 - 1) as i:
                    tanhs(i * 2 + 2, 0)
                    tanhs(i * 2 + 3, 1)
                tanhs(KEYS - 1, 0)
                act.wait_ge(rho_shifted, 1)
                nc.scalar.activation(rho, rho, ACT.Exp).then_inc(rho_exp, 1)
                act.wait_ge(gate_sums, 1)
                for w in range(2):
                    last = nc.scalar.activation(fcol[:, 4 + w, :], fcol[:, 2 + w, :], ACT.Tanh, bias=scal_bias[:, w:w + 1])
                last.then_inc(gate_tanh, 1)
                end_phase(act, "act")

            if STOP_AFTER >= 4:
                begin_phase(act, "act", 3)
                take_transposes(2)
                act.wait_ge(moe_gates_psum, 1)
                nc.scalar.activation(gates.rearrange("p (c a) e -> p c (a e)", c=2), ps[:, 4:6, :],
                                     ACT.Sigmoid).then_inc(moe_sigmoid, 1)
                units = [(b, i, h) for b in range(B) for i in range(TILES // 2) for h in range(2)]
                act.wait_ge(dist_in, 32)
                act.wait_ge(tb_in, 16)
                with act.Fori(0, 4) as hp:
                    for u in range(8):
                        q, which = divmod(u, 2)
                        act.wait_ge(qk_psum, hp * 8 + (u + 1))
                        dst = (QT if which == 0 else KT)[:, :, q * 256:(q + 1) * 256].rearrange("p b (j n) -> p b j n", n=P)
                        nc.scalar.mul(dst, ps[:, u % 4, :].rearrange("p (j b n) -> p b j n", b=B, n=P),
                                      0.125 if which == 0 else 1.0).then_inc(qk_ready, 1)
                    for k in range(8):
                        act.wait_ge(relu_used, hp * 8 + (k + 1))
                        nc.scalar.activation(relu_ring[:, k % 2, :], dist, ACT.Relu, bias=tb[:, bass.ds(hp * 8 + (32 + k), 1)],
                                             scale=tb[:, bass.ds(hp * 8 + k, 1)]).then_inc(relu_ready, 1)

                    def exponentials(u):
                        b, i, h = units[u]
                        act.wait_ge(s_max, hp * 32 + (u + 1))
                        n = (i + 1) * P
                        if n <= GT:
                            nc.scalar.activation(P_sb[:, u % 2, 0:n], ps[:, 0, 0:n], ACT.Exp, bias=acol[:, u % 2, 0:1],
                                                 accum_out=acol[:, u % 2, 1:2]).then_inc(s_exp, 1)
                        else:
                            nc.scalar.activation(P_sb[:, u % 2, 0:n], ps[:, 0:2, :].rearrange("p a n -> p (a n)")[:, 0:n],
                                                 ACT.Exp, bias=acol[:, u % 2, 0:1],
                                                 accum_out=acol[:, u % 2, 1:2]).then_inc(s_exp, 1)

                    def take_mixT(u):
                        b, i, h = units[u]
                        act.wait_ge(pT_psum, hp * 32 + (u + 1))
                        n = (i + 1) * P
                        cp(PT_sb[:, u % 2, 0:i + 1, :].rearrange("p j n -> p (j n)"),
                           ps[:, 2:4, :].rearrange("p a n -> p (a n)")[:, 0:n]).then_inc(pT_ready, 1)

                    def take_gatedT(u):
                        act.wait_ge(gT_psum, hp * 32 + (u + 1))
                        cp(GT_sb[:, u % 2, :, :].rearrange("p j n -> p (j n)"), ps[:, 5, :]).then_inc(gT_ready, 1)

                    for u in range(len(units) + 2):
                        if 1 <= u <= len(units):
                            take_mixT(u - 1)
                        if u >= 2:
                            take_gatedT(u - 2)
                        if u < len(units):
                            exponentials(u)
                end_phase(act, "act")

            if STOP_AFTER >= 5:
                def decoder_layer(l, last=False):
                    begin_phase(act, "act", l * 2 + 4)
                    context_attention(TIMED, l * 16 + 16, l)
                    end_phase(act, "act")
                    begin_phase(act, "act", l * 2 + 5)
                    act.wait_ge(ff_w_in, l * 64 + 64)
                    if not last:
                        act.wait_ge(tb_in, l * 16 + 32)

                    def transposed(q):
                        act.wait_ge(gnT_psum, l * 4 + (q + 1))
                        for c in range(2):
                            last = cp(gT[:, q % 2, :, c * 256:(c + 1) * 256],
                                      ps[:, 4 + c, :].rearrange("p (k n) -> p k n", k=KC))
                        last.then_inc(gnT_ready, 1)

                    transposed(0)
                    for q in range(GROUPS):
                        for m in range(8):
                            act.wait_ge(hid_psum, l * 32 + (q * 8 + m + 1))
                            nc.scalar.activation(hidT[:, m, :], ps[:, m % 4, :], ACT.Relu, bias=b_f1[:, m:m + 1]).then_inc(hid_ready, 1)
                            if last:
                                continue
                            k = 8 * q + m
                            act.wait_ge(relu_used, l * 32 + (33 + k))
                            nc.scalar.activation(relu_ring[:, k % 2, :], dist, ACT.Relu, bias=tb[:, 32 + k:33 + k],
                                                 scale=tb[:, k:k + 1]).then_inc(relu_ready, 1)
                        if q + 1 < GROUPS:
                            transposed(q + 1)
                    end_phase(act, "act")

                with act.Fori(0, LAYERS - 1) as l:
                    decoder_layer(l)
                decoder_layer(LAYERS - 1, last=True)
                end_phase(act, "act")

            if STOP_AFTER >= 6:
                begin_phase(act, "act", 13)
                take_transposes(3, pairT3)
                end_phase(act, "act")

            if STOP_AFTER >= 7:
                begin_phase(act, "act", 14)
                context_attention(SWISH, 80)
                end_phase(act, "act")

            if STOP_AFTER >= 8:
                begin_phase(act, "act", 15)
                take_transposes(4, pairT)
                router_exponentials(1)
                expert_tiles(GELU)
                end_phase(act, "act")

        @block.vector
        def _(dve):
            v = nc.vector
            tt, ts, red = v.tensor_tensor, v.tensor_scalar, v.tensor_reduce

            def tile(buf, t):
                return buf[:, t, :] if isinstance(t, int) else buf[:, bass.ds(t, 1), :].rearrange("p a d -> p (a d)")

            def norm_stats(src, t, slot, kind):
                v.bn_stats(stats[:, slot, :], tile(src, t))
                dve.drain()
                v.bn_aggr(mv[:, slot, :], stats[:, slot, :])
                dve.drain()
                ts(pow_in[:, slot:slot + 1], mv[:, slot, 1:2], 1e-5 if kind == LN else 0.0, None,
                   ALU.add).then_inc(var_ready, 1)

            def norm_apply(src, dst, t, slot, kind, ring):
                dve.wait_ge(rstd_ready, ring + t + 1)
                if kind == DECODER:
                    ts(rstd[:, slot:slot + 1], rstd[:, slot:slot + 1], 1e-6, None, ALU.add)
                    dve.drain()
                    v.reciprocal(rstd[:, slot:slot + 1], rstd[:, slot:slot + 1])
                    dve.drain()
                ts(dst, tile(src, t), mv[:, slot, 0:1], rstd[:, slot:slot + 1], ALU.subtract,
                   ALU.mult).then_inc(xn_ready, 1)

            def context_attention(cfg, stream, kind, ring, layer=0):
                n, kv, fold, att = plan(cfg, layer)
                m0 = 0 if cfg.hpc == 8 else 8
                for cc in range(2 * cfg.chunks):
                    dve.wait_ge(bd_psum, kv + cc + 1)
                    bd = view(bd_off + (cc % 2) * B * 616, B, cfg.hpc * KEYS)
                    for h in range(cfg.hpc):
                        last = ts(bd[:, :, h * KEYS:(h + 1) * KEYS],
                                  ps[:, cc % 2, 0:B * KEYS].rearrange("p (b k) -> p b k", b=B),
                                  bd_mask[:, m0 + h:m0 + h + 1], None, ALU.mult)
                    last.then_inc(bd_ready, 1)

                def stats_of(t, s):
                    norm_stats(stream, t, s, kind)

                def apply_to(t, s, fresh=False):
                    if not fresh:
                        dve.wait_ge(xnT_psum, ring + t - 1)
                    norm_apply(stream, xn[:, s, :], t, s, kind, ring)

                def shift(t, s):
                    dve.wait_ge(logits_ready, att + t + 1)
                    sh = shifted[:, s, :]
                    for run in cfg.runs:
                        lb = logit_banks(cfg, run)
                        if cfg.kind == "masked":
                            tt(lb, lb, bias_rows(tile(keep, t), run), ALU.mult)
                    if cfg.kind == "masked":
                        dve.drain()
                    for run in cfg.runs:
                        lb = logit_banks(cfg, run)
                        if cfg.kind == "swish":
                            tt(head_cols(raw_logits[:, s, :], cfg, run), lb,
                               head_cols(cbias[:, s, :], cfg, run), ALU.add)
                        else:
                            tt(lb, lb, bias_rows(tile(negm, t), run), ALU.add)
                    dve.drain()
                    for run in cfg.runs:
                        src = logit_banks(cfg, run) if cfg.kind != "swish" else head_cols(raw_logits[:, s, :], cfg, run)
                        red(head_scal(mx[:, s, :], cfg, run, False), src, AXX, ALU.max)
                    dve.drain()
                    for run in cfg.runs:
                        src = logit_banks(cfg, run) if cfg.kind != "swish" else head_cols(raw_logits[:, s, :], cfg, run)
                        last = tt(head_cols(sh, cfg, run), src, head_scal(mx[:, s, :], cfg, run, True), ALU.subtract)
                    last.then_inc(shifted_ready, 1)

                def row_sums(t, s):
                    dve.wait_ge(exp_ready, att + t + 1)
                    pr = probs[:, s, 0:cfg.cols].rearrange("p (h k) -> p h k", k=KEYS)
                    if cfg.kind == "swish":
                        rw = raw_logits[:, s, 0:cfg.cols].rearrange("p (h k) -> p h k", k=KEYS)
                        tt(pr, pr, rw, ALU.mult)
                        dve.drain()
                        red(rsum[:, s, 0:cfg.heads], pr, AXX, ALU.add, apply_absolute_value=True)
                        dve.drain()
                        ts(rsum[:, s, 0:cfg.heads], rsum[:, s, 0:cfg.heads], 1.0, None, ALU.add)
                    else:
                        red(rsum[:, s, 0:cfg.heads], pr, AXX, ALU.add)
                    dve.drain()
                    v.reciprocal(rinv[:, s, 0:cfg.heads], rsum[:, s, 0:cfg.heads]).then_inc(rinv_ready, 1)

                def update(t, s):
                    dve.wait_ge(att_out, att + t + 1)
                    if cfg.kind == "masked":
                        tt(tile(stream, t), tile(stream, t), cols_bo, ALU.add)
                        dve.drain()
                    tt(tile(stream, t), ps[:, 7, 0:D], tile(stream, t), ALU.add).then_inc(x_updated, 1)

                stats_of(0, 0)
                stats_of(1, 1)
                apply_to(0, 0, fresh=True)
                apply_to(1, 1, fresh=True)
                dve.wait_ge(fold_v_saved, n * 32 + 32)

                def step(t, s, lead=True):
                    if lead:
                        stats_of(t + 2, s)
                    shift(t, s)
                    if lead:
                        apply_to(t + 2, s)
                    row_sums(t, s)

                step(0, 0)
                step(1, 1)
                update(0, 0)
                with dve.Fori(0, 6) as i:
                    for d, s in ((2, 0), (3, 1)):
                        step(i * 2 + d, s)
                        update(i * 2 + d - 1, 1 - s)
                step(14, 0, lead=False)
                update(13, 1)
                step(15, 1, lead=False)
                update(14, 0)
                update(15, 1)

            dve.wait_ge(consts_in, 112)
            dve.wait_ge(x_in, 16)
            dve.wait_ge(mask_in, 16)
            ts(keep.rearrange("p t k -> p (t k)"), mask_i, 0, None, ALU.not_equal)
            ts(negm.rearrange("p t k -> p (t k)"), mask_i, 0, -2.5e9, ALU.is_equal, ALU.mult)
            dve.wait_ge(consts_made, 2)
            context_attention(MASKED, x, LN, 0)
            end_phase(dve, "dve")

            def batch_statistics(src, kind, n):
                with dve.Fori(0, 4) as q:
                    for j in range(4):
                        v.bn_stats(stats[:, j, :], tile(src, q * 4 + j))
                    dve.drain()
                    for j in range(4):
                        v.bn_aggr(mv4[:, j, :], stats[:, j, :])
                    dve.drain()
                    v.tensor_copy(mv[:, bass.ds(q * 4, 4), :], mv4)
                    dve.drain()
                ts(pow_in, mv[:, :, 1:2].rearrange("p t a -> p (t a)"), 1e-5 if kind == LN else 0.0, None,
                   ALU.add).then_inc(all_var_ready, 1)
                dve.wait_ge(all_rstd_ready, n + 1)
                if kind == DECODER:
                    ts(rstd, rstd, 1e-6, None, ALU.add)
                    dve.drain()
                    v.reciprocal(rstd, rstd)
                    dve.drain()

            def normalise_all(src, dst, n):
                batch_statistics(src, LN, n)
                for t in range(TILES):
                    ts(dst[:, t, :], src[:, t, :], mv[:, t, 0:1], rstd[:, t:t + 1], ALU.subtract,
                       ALU.mult).then_inc(all_xn_ready, 1)

            def first_of(dst, values, peak):
                tt(dst, values, peak.unsqueeze(2).broadcast_to([P, TILES, EXPERTS]), ALU.is_equal)
                dve.drain()
                tt(dst, dst, later8.unsqueeze(1).broadcast_to([P, TILES, EXPERTS]), ALU.mult)
                dve.drain()
                red(rcol[:, 2, :], dst, AXX, ALU.max)
                dve.drain()
                tt(dst, dst, rcol[:, 2, :].unsqueeze(2).broadcast_to([P, TILES, EXPERTS]), ALU.is_equal)
                dve.drain()

            def route_tokens(r, choices, slot_tiles):
                per_tile = lambda c: c.unsqueeze(2).broadcast_to([P, TILES, EXPERTS])
                per_expert = lambda c: c.unsqueeze(1).broadcast_to([P, TILES, EXPERTS])
                shifted_, probs_, chosen, one = route[0], route[1], route[2], [route[3], route[4]]
                total, run_, pos = route[5], route[6], route[7]
                logits = ps[:, 5, 0:P].rearrange("p (t e) -> p t e", e=EXPERTS)
                dve.wait_ge(router_ready, r + 1)
                red(rcol[:, 0, :], logits, AXX, ALU.max)
                dve.drain()
                tt(shifted_, logits, per_tile(rcol[:, 0, :]), ALU.subtract).then_inc(router_shifted, 1)
                dve.wait_ge(router_exp, r + 1)
                red(rcol[:, 0, :], probs_, AXX, ALU.add)
                dve.drain()
                v.reciprocal(rcol[:, 1, :], rcol[:, 0, :])
                dve.drain()
                tt(probs_, probs_, per_tile(rcol[:, 1, :]), ALU.mult)
                dve.drain()
                for c in range(choices):
                    red(score[:, c, :], probs_, AXX, ALU.max)
                    dve.drain()
                    first_of(one[c], probs_, score[:, c, :])
                    if c + 1 < choices:
                        v.scalar_tensor_tensor(probs_, one[c], -2.0, probs_, ALU.mult, ALU.add)
                        dve.drain()
                if choices == 2:
                    tt(chosen, one[0], one[1], ALU.add).then_inc(chosen_ready, 1)
                else:
                    v.tensor_copy(chosen, one[0]).then_inc(chosen_ready, 1)
                dve.wait_ge(ranks_ready, r + 1)
                v.tensor_copy(total, ps[:, 4, 0:P].rearrange("p (t e) -> p t e", e=EXPERTS))
                dve.drain()
                src, dst = total, run_
                for d in (1, 2, 4, 8):
                    tt(dst[:, d:, :], src[:, d:, :], src[:, 0:TILES - d, :], ALU.add)
                    v.tensor_copy(dst[:, 0:d, :], src[:, 0:d, :])
                    dve.drain()
                    src, dst = dst, (shifted_ if dst is run_ else run_)
                running = src
                count, tiles_e, e0, e1 = (small8[:, k, :] for k in range(4))
                ci = small8[:, 4, :].bitcast(INT32)
                ts(ci, running[:, TILES - 1, :], 127.0, None, ALU.add)
                dve.drain()
                ts(ci, ci, 7, None, ALU.arith_shift_right)
                dve.drain()
                v.tensor_copy(tiles_e, ci)
                dve.drain()
                src, dst = tiles_e, e0
                for d in (1, 2, 4):
                    tt(dst[:, d:], src[:, d:], src[:, 0:EXPERTS - d], ALU.add)
                    v.tensor_copy(dst[:, 0:d], src[:, 0:d])
                    dve.drain()
                    src, dst = dst, (e1 if dst is e0 else e0)
                ends_e = src
                tt(count, ends_e, tiles_e, ALU.subtract)
                te = tile_expert_f[:, 0:slot_tiles, :]
                tt(te, ends_e.unsqueeze(1).broadcast_to([P, slot_tiles, EXPERTS]),
                   tile_of[:, 0:slot_tiles].unsqueeze(2).broadcast_to([P, slot_tiles, EXPERTS]), ALU.is_le)
                dve.drain()
                red(tile_of_expert[:, 0:slot_tiles], te, AXX, ALU.add)
                dve.drain()
                ts(tile_expert[:, 0:slot_tiles], tile_of_expert[:, 0:slot_tiles], float(EXPERTS - 1), None, ALU.min)
                tt(pos, running, total, ALU.subtract)
                dve.drain()
                tt(pos, pos, ps[:, 3, 0:P].rearrange("p (t e) -> p t e", e=EXPERTS), ALU.add)
                ts(count, count, float(P), None, ALU.mult)
                dve.drain()
                tt(pos, pos, per_expert(count), ALU.add)
                dve.drain()
                for c in range(choices):
                    tt(one[c], one[c], pos, ALU.mult)
                dve.drain()
                for c in range(choices):
                    red(slot_f[:, c, :], one[c], AXX, ALU.add)
                dve.drain()
                v.tensor_copy(slot_i[:, 0:choices, :], slot_f[:, 0:choices, :]).then_inc(slots_ready, 1)

            def expert_tiles(run):
                b = run.base
                ff_h = ff_h_gelu if run.kind == "gelu" else ff_h_swiglu

                def raise_(t, slot):
                    if run.kind == "gelu":
                        dve.wait_ge(ff_up, b + t + 1)
                        dve.wait_ge(ff_bias_in[slot], ring_uses(t, slot) * 2)
                        tt(ff_h[:, slot, :].rearrange("p (a n) -> p a n", a=2), ps[:, 1:3, :],
                           ff_b1[:, slot, :].rearrange("p (a n) -> p a n", a=2), ALU.add).then_inc(ff_biased, 1)
                    else:
                        dve.wait_ge(ff_gate, b + t + 1)
                        tt(ff_h[:, slot, 0:256], ff_h[:, slot, 512:768], ps[:, 1, 256:512], ALU.mult).then_inc(ff_h_ready, 1)

                def result(t, slot, fresh=False):
                    dve.wait_ge(ff_y_psum, b + t + 1)
                    if run.kind == "shared":
                        tt(tile(x, t), ps[:, 5, 0:D], tile(x, t), ALU.add).then_inc(ff_y_ready, 1)
                        return
                    if not fresh:
                        dve.wait_ge(ff_y_stored[slot], ring_uses(t, slot) - 16 + run.stored * 8)
                    if run.kind == "gelu":
                        tt(ff_y[:, slot, :], ps[:, 5, 0:D], ff_b2[:, slot, :], ALU.add).then_inc(ff_y_ready, 1)
                    else:
                        v.tensor_copy(ff_y[:, slot, :], ps[:, 5, 0:D]).then_inc(ff_y_ready, 1)

                raise_(0, 0)
                raise_(1, 1)
                result(0, 0, fresh=True)
                raise_(2, 0)
                result(1, 1, fresh=True)
                with dve.Fori(0, run.tiles // 2 - 2) as i:
                    for d, s in ((3, 1), (4, 0)):
                        raise_(i * 2 + d, s)
                        result(i * 2 + d - 1, 1 - s)
                raise_(run.tiles - 1, 1)
                result(run.tiles - 2, 0)
                result(run.tiles - 1, 1)

            if STOP_AFTER >= 2:
                begin_phase(dve, "dve", 1)
                normalise_all(x, z, 0)
                dve.wait_ge(route_consts_in, 64)
                route_tokens(0, 2, SLOT_TILES)
                for t in range(TILES):
                    for c in range(2):
                        u = 2 * t + c
                        if t >= 1:
                            dve.wait_ge(row_scattered[c], t * 16)
                        ts(rows_ring[:, c, :], z[:, t, :], score[:, c, t:t + 1], None, ALU.mult).then_inc(row_scaled, 1)
                expert_tiles(SHARED)
                expert_tiles(SWIGLU)
                for t in range(TILES):
                    for c in range(2):
                        dve.wait_ge(row_gathered[c], (t + 1) * 16)
                        tt(x[:, t, :], x[:, t, :], rows_ring[:, c, :], ALU.add).then_inc(row_added, 1)
                        dve.wait_ge(row_added, 2 * t + c + 1)
                end_phase(dve, "dve")

            if STOP_AFTER >= 3:
                begin_phase(dve, "dve", 2)
                dve.wait_ge(add_w_in, 96)
                for w in range(2):
                    for k in range(KC):
                        last = v.tensor_copy(gate_rep[:, w, k, :],
                                             gate_cols[:, 2 + 2 * w + k:3 + 2 * w + k].broadcast_to([P, P]))
                v.memset(w_col, 0.0)
                dve.drain()
                last = v.tensor_copy(w_col[:, :, 0:1].rearrange("p m a -> p (m a)"), gate_cols[:, 0:2])
                last.then_inc(rep_ready, 1)
                ts(q_mask, q_mask_i, -1.0, 1.0, ALU.mult, ALU.add)
                dve.drain()
                ts(q_mask, q_mask, -1e30, None, ALU.mult)
                dve.wait_ge(text_psum, 1)
                for m in range(KC):
                    ts(textT[:, m, :], ps[:, 4, m * 154:(m + 1) * 154], add_bias[:, m:m + 1], None, ALU.add)
                v.tensor_copy(gate_txt.rearrange("p a b -> p (a b)"), ps[:, 5, 0:308]).then_inc(text_ready, 1)
                normalise_all(x, z, 1)
                for pair in range(TILES // 2):
                    dve.wait_ge(feat_psum, pair + 1)
                    for m in range(KC):
                        last = v.tensor_copy(featT[:, m, :, pair * P:(pair + 1) * P],
                                             ps[:, 2 * (pair % 2) + m, 0:256].rearrange("p (b n) -> p b n", b=B))
                    last.then_inc(feat_ready, 1)
                def take_scores(t, slot, fresh=False):
                    dve.wait_ge(rho_psum, t + 1)
                    if not fresh:
                        dve.wait_ge(rho_stored[slot], ring_uses(t, slot) - 16)
                    v.tensor_copy(score_rows[:, slot, :], ps[:, slot, :]).then_inc(rho_taken, 1)

                take_scores(0, 0, fresh=True)
                take_scores(1, 1, fresh=True)
                with dve.Fori(0, KEYS // 2 - 1) as i:
                    take_scores(i * 2 + 2, 0)
                    take_scores(i * 2 + 3, 1)
                take_scores(KEYS - 1, 0)
                dve.wait_ge(rhoT_psum, 1)
                for c, w in ((0, 6), (1, 6), (2, 4)):
                    v.tensor_copy(rho[:, 6 * c:6 * c + w, :].rearrange("p j k -> p (j k)"), ps[:, 2 + c, 0:w * KEYS])
                dve.drain()
                for b in range(B):
                    tt(rho[:, 8 * b:8 * b + 8, :], rho[:, 8 * b:8 * b + 8, :],
                       q_mask[:, b * KEYS:(b + 1) * KEYS].unsqueeze(1).broadcast_to([P, 8, KEYS]), ALU.add)
                dve.drain()
                red(fcol[:, 0, :], rho, AXX, ALU.max)
                dve.drain()
                per_tile = lambda c: c.unsqueeze(2).broadcast_to([P, TILES, KEYS])
                tt(rho, rho, per_tile(fcol[:, 0, :]), ALU.subtract).then_inc(rho_shifted, 1)
                dve.wait_ge(rho_exp, 1)
                red(fcol[:, 0, :], rho, AXX, ALU.add)
                dve.drain()
                v.reciprocal(fcol[:, 1, :], fcol[:, 0, :])
                for w in range(2):
                    for b in range(B):
                        tt(rho2[:, 8 * b:8 * b + 8, :], rho[:, 8 * b:8 * b + 8, :],
                           gate_txt[:, w, b * KEYS:(b + 1) * KEYS].unsqueeze(1).broadcast_to([P, 8, KEYS]), ALU.mult)
                    dve.drain()
                    red(fcol[:, 2 + w, :], rho2, AXX, ALU.add)
                    dve.drain()
                    last = tt(fcol[:, 2 + w, :], fcol[:, 2 + w, :], fcol[:, 1, :], ALU.mult)
                last.then_inc(gate_sums, 1)
                dve.wait_ge(gate_tanh, 1)
                for t in range(TILES):
                    c = (t % 2) * 8 + t // 2
                    ts(add_tmp[:, t % 2, :], z[:, t, :], fcol[:, 4, c:c + 1], fcol[:, 5, c:c + 1], ALU.mult, ALU.add)
                    dve.drain()
                    tt(x[:, t, :], x[:, t, :], add_tmp[:, t % 2, :], ALU.add)
                end_phase(dve, "dve")

            if STOP_AFTER >= 4:
                begin_phase(dve, "dve", 3)
                normalise_all(x, z, 2)
                dve.wait_ge(moe_sigmoid, 1)
                each = lambda c: c.unsqueeze(2).broadcast_to([P, TILES * 8, 8])
                red(gpeak[:, 0, :], gates, AXX, ALU.max)
                dve.drain()
                tt(gsel, gates, each(gpeak[:, 0, :]), ALU.is_equal)
                dve.drain()
                tt(gsel, gsel, later8.unsqueeze(1).broadcast_to([P, TILES * 8, 8]), ALU.mult)
                dve.drain()
                red(gpeak[:, 1, :], gsel, AXX, ALU.max)
                dve.drain()
                tt(gsel, gsel, each(gpeak[:, 1, :]), ALU.is_equal)
                dve.drain()
                tt(gates, gates, gsel, ALU.mult).then_inc(moe_gates_ready, 1)
                dve.drain()
                dve.sem_inc(y_taken, 1)
                units = [(b, i, h) for b in range(B) for i in range(TILES // 2) for h in range(2)]
                with dve.Fori(0, 4) as hp:
                    v.tensor_copy(pair_gates, gates.rearrange("p (t h) e -> p t (h e)", t=TILES)[:, :, bass.ds(hp * 16, 16)])
                    dve.drain()

                    def gate_of(t, h):
                        return pair_gates[:, t, h * 8:h * 8 + 8]

                    for w in range(32):
                        t, h = divmod(w, 2)
                        dve.wait_ge(v_psum, hp * 32 + (w + 1))
                        tt(v_tmp[:, w % 2, :, :], ps[:, 4 + w % 4, :].rearrange("p (e k) -> p e k", k=64),
                           gate_of(t, h).unsqueeze(2).broadcast_to([P, 8, 64]), ALU.mult).then_inc(v_gated, 1)
                        dve.drain()
                        red(V[:, t, h, :], v_tmp[:, w % 2, :, :].rearrange("p e k -> p k e"), AXX, ALU.add).then_inc(v_ready, 1)

                    def maximum(u):
                        b, i, h = units[u]
                        dve.wait_ge(s_psum, hp * 32 + (u + 1))
                        c = (i % 4) * P
                        tt(ps[:, i // 4, c:c + P], ps[:, i // 4, c:c + P], tri, ALU.add)
                        dve.drain()
                        n = (i + 1) * P
                        src = ps[:, 0, 0:n] if n <= GT else ps[:, 0:2, :].rearrange("p a n -> p (a n)")[:, 0:n]
                        red(acol[:, u % 2, 0:1], src, AXX, ALU.max, negate=True).then_inc(s_max, 1)

                    def gate(u):
                        b, i, h = units[u]
                        dve.wait_ge(s_exp, hp * 32 + (u + 1))
                        v.reciprocal(acol[:, u % 2, 2:3], acol[:, u % 2, 1:2])
                        dve.drain()
                        ts(acol[:, u % 2, 8:16], gate_of(2 * i + b, h), acol[:, u % 2, 2:3], None, ALU.mult)
                        dve.drain()
                        dve.wait_ge(o_psum, hp * 32 + (u + 1))
                        tt(G_sb[:, u % 2, :].rearrange("p (e k) -> p e k", k=64),
                           ps[:, 4, 64 * h:64 * h + 64].unsqueeze(1).broadcast_to([P, 8, 64]),
                           acol[:, u % 2, 8:16].unsqueeze(2).broadcast_to([P, 8, 64]), ALU.mult).then_inc(g_ready, 1)

                    def update(u):
                        b, i, h = units[u]
                        dve.wait_ge(y_psum, hp * 16 + (u // 2 + 1))
                        t = 2 * i + b
                        tt(x[:, t, :], ps[:, 6 + (u // 2) % 2, 0:D], x[:, t, :], ALU.add).then_inc(y_taken, 1)

                    for u in range(len(units) + 2):
                        if u < len(units):
                            maximum(u)
                        if 1 <= u <= len(units):
                            gate(u - 1)
                        if u >= 2 and units[u - 2][2] == 1:
                            update(u - 2)
                end_phase(dve, "dve")

            if STOP_AFTER >= 5:
                begin_phase(dve, "dve", 4)
                normalise_all(x, z, 3)
                def decoder_layer(l, final=False):
                    begin_phase(dve, "dve", l * 2 + 4)
                    dve.wait_ge(relu_used, l * 32 + 34)
                    context_attention(TIMED, z, DECODER, l * 16 + 16, l)
                    end_phase(dve, "dve")
                    begin_phase(dve, "dve", l * 2 + 5)
                    dve.wait_ge(ff_w_in, l * 64 + 64)
                    if not final:
                        dve.wait_ge(tb_in, l * 16 + 32)

                    def time_bias(q):
                        if q == 0:
                            ts(qbias.rearrange("p (j c) -> p j c", c=B * KEYS),
                               ff0.unsqueeze(1).broadcast_to([P, TILES // 2, B * KEYS]), tb[:, 96:97], None, ALU.add)
                            dve.drain()
                        for k in range(8 * q, 8 * q + 8):
                            dve.wait_ge(relu_ready, l * 32 + (33 + k))
                            v.scalar_tensor_tensor(qbias, relu_ring[:, k % 2, :], tb[:, 64 + k:65 + k], qbias,
                                                   ALU.mult, ALU.add).then_inc(relu_used, 1)
                            dve.drain()

                    def group_stats(q):
                        for j in range(4):
                            v.bn_stats(stats[:, j, :], z[:, 4 * q + j, :])
                        dve.drain()
                        for j in range(4):
                            v.bn_aggr(mv4[:, j, :], stats[:, j, :])
                        dve.drain()
                        v.tensor_copy(pow_in[:, 0:4], mv4[:, :, 1:2].rearrange("p t a -> p (t a)")).then_inc(gn_var, 1)

                    def group_apply(q):
                        dve.wait_ge(gn_rstd, l * 4 + (q + 1))
                        ts(rstd[:, 0:4], rstd[:, 0:4], 1e-6, None, ALU.add)
                        dve.drain()
                        v.reciprocal(rstd[:, 0:4], rstd[:, 0:4])
                        dve.drain()
                        if q >= 1:
                            dve.wait_ge(gnT_psum, l * 4 + q)
                        for j in range(4):
                            last = ts(xng[:, j, :], z[:, 4 * q + j, :], mv4[:, j, 0:1], rstd[:, j:j + 1],
                                      ALU.subtract, ALU.mult)
                        last.then_inc(gn_ready, 1)

                    group_stats(0)
                    group_apply(0)
                    for q in range(GROUPS):
                        if q + 1 < GROUPS:
                            group_stats(q + 1)
                            group_apply(q + 1)
                        if not final:
                            time_bias(q)
                        for c in range(2):
                            dve.wait_ge(down_psum, l * 8 + (2 * q + c + 1))
                            bank = ps[:, 6 + c, :].rearrange("p (t d) -> p t d", d=D)
                            tt(bank, bank, b_f2.unsqueeze(1).broadcast_to([P, 2, D]), ALU.add)
                            dve.drain()
                            rows = z[:, 4 * q + 2 * c:4 * q + 2 * c + 2, :]
                            tt(rows, bank, rows, ALU.add).then_inc(down_taken, 1)
                    end_phase(dve, "dve")

                with dve.Fori(0, LAYERS - 1) as l:
                    decoder_layer(l)
                decoder_layer(LAYERS - 1, final=True)
                begin_phase(dve, "dve", 12)
                batch_statistics(z, DECODER, 4)
                for t in range(TILES):
                    ts(z[:, t, :], z[:, t, :], mv[:, t, 0:1], rstd[:, t:t + 1], ALU.subtract, ALU.mult)
                dve.drain()
                for t in range(0, TILES, 4):
                    tt(x[:, t:t + 4, :], x[:, t:t + 4, :], z[:, t:t + 4, :], ALU.add)
                end_phase(dve, "dve")

            if STOP_AFTER >= 6:
                begin_phase(dve, "dve", 13)
                dve.wait_ge(sign_in, 16)
                ts(w_sign, w_raw, 0.0, None, ALU.is_gt)
                ts(w_neg, w_raw, 0.0, None, ALU.is_lt)
                dve.drain()
                tt(w_sign, w_sign, w_neg, ALU.subtract).then_inc(sign_ready, 1)
                normalise_all(x, z, 5)
                for pair in range(TILES // 2):
                    dve.wait_ge(sign_psum, pair + 1)
                    rows = x[:, 2 * pair:2 * pair + 2, :]
                    tt(rows, ps[:, pair % 2, :].rearrange("p (t d) -> p t d", d=D), rows, ALU.add).then_inc(sign_taken, 1)
                end_phase(dve, "dve")

            if STOP_AFTER >= 7:
                begin_phase(dve, "dve", 14)
                dve.wait_ge(head_bias_in, 16)
                for c in range(SWISH.chunks):
                    last = v.tensor_copy(head_bias_rep[:, c, :], head_bias[:, c:c + 1].broadcast_to([P, P]))
                last.then_inc(bias_rep_ready, 1)
                context_attention(SWISH, x, LN, 80)
                end_phase(dve, "dve")

            if STOP_AFTER >= 8:
                begin_phase(dve, "dve", 15)
                dve.wait_ge(route_consts_in, 144)
                tt(wg_sq, wg, wg, ALU.mult)
                dve.drain()
                red(wg_col[:, 0:1], wg_sq, AXX, ALU.add).then_inc(wg_square, 1)
                dve.wait_ge(wg_norm, 1)
                ts(wg_col[:, 2:3], wg_col[:, 1:2], 1e-4, None, ALU.max)
                dve.drain()
                v.reciprocal(wg_col[:, 3:4], wg_col[:, 2:3])
                dve.drain()
                ts(wg, wg, wg_col[:, 3:4], None, ALU.mult).then_inc(wg_ready, 1)
                dve.wait_ge(wgT_psum, 1)
                v.tensor_copy(wgT, ps[0:16, 2, 0:8]).then_inc(wgT_ready, 1)
                dve.wait_ge(w_router_psum, 1)
                v.tensor_copy(w_router.rearrange("p k e -> p (k e)"), ps[:, 2, 16:32]).then_inc(w_router_ready, 1)
                normalise_all(x, z, 6)
                route_tokens(1, 1, GELU.tiles)
                expert_tiles(GELU)
                for t in range(TILES):
                    c = t % 2
                    dve.wait_ge(row_gathered[c], (TILES + t // 2 + 1) * 16)
                    v.scalar_tensor_tensor(x[:, t, :], rows_ring[:, c, :], score[:, 0, t:t + 1], x[:, t, :],
                                           ALU.mult, ALU.add).then_inc(row_added, 1)
                end_phase(dve, "dve")

        @block.gpsimd
        def _(pool):
            g = nc.gpsimd
            g.memset(minus_half, -0.5).then_inc(consts_made, 1)
            g.memset(plus_half, 0.5).then_inc(consts_made, 1)
            g.memset(zero_row, 0.0).then_inc(zeros_made, 1)
            pool.drain()

            def norm_root(t, slot, kind, ring):
                pool.wait_ge(var_ready, ring + t + 1)
                g.tensor_tensor(rstd[:, slot:slot + 1], pow_in[:, slot:slot + 1],
                                (minus_half if kind == LN else plus_half)[:, 0:1], ALU.pow).then_inc(rstd_ready, 1)

            def context_attention(cfg, kind, ring, layer=0):
                n, kv, fold, att = plan(cfg, layer)

                def normalise(t, s):
                    pool.wait_ge(rinv_ready, att + t + 1)
                    pr = probs[:, s, 0:cfg.cols].rearrange("p (h k) -> p h k", k=KEYS)
                    g.tensor_tensor(pr, pr, rinv[:, s, 0:cfg.heads].unsqueeze(2).broadcast_to([P, cfg.heads, KEYS]),
                                    ALU.mult).then_inc(probs_ready, 1)

                norm_root(0, 0, kind, ring)
                norm_root(1, 1, kind, ring)
                with pool.Fori(0, 7) as i:
                    for s in range(2):
                        norm_root(i * 2 + s + 2, s, kind, ring)
                        normalise(i * 2 + s, s)
                normalise(14, 0)
                normalise(15, 1)

            context_attention(MASKED, LN, 0)
            end_phase(pool, "pool")

            def time_bias(base, k0, count=8):
                if k0 == 0:
                    g.tensor_scalar(qbias.rearrange("p (j c) -> p j c", c=B * KEYS),
                                    ff0.unsqueeze(1).broadcast_to([P, TILES // 2, B * KEYS]), tb[:, 96:97], None, ALU.add)
                    pool.drain()
                for k in range(k0, k0 + count):
                    pool.wait_ge(relu_ready, base + (k + 1))
                    g.tensor_tensor(relu_ring[:, k % 2, :], relu_ring[:, k % 2, :],
                                    tb[:, 64 + k:65 + k].broadcast_to([P, TILES * KEYS]), ALU.mult)
                    pool.drain()
                    g.tensor_tensor(qbias, qbias, relu_ring[:, k % 2, :], ALU.add).then_inc(relu_used, 1)
                    pool.drain()

            def batch_root(n, kind):
                pool.wait_ge(all_var_ready, n + 1)
                g.tensor_tensor(rstd, pow_in, minus_half if kind == LN else plus_half, ALU.pow).then_inc(all_rstd_ready, 1)

            def scatter(t, c, index):
                g.indirect_dma_start(slots_x[index], bass.IndirectOffsetOnAxis(slot_i[:, c, t:t + 1], 0),
                                     rows_ring[:, c, :] if index == 0 else z[:, t, :], None).then_inc(row_scattered[c], 16)

            def gather(t, c, index):
                g.indirect_dma_start(rows_ring[:, c, :], None, slots_y[index],
                                     bass.IndirectOffsetOnAxis(slot_i[:, c, t:t + 1], 0)).then_inc(row_gathered[c], 16)

            if STOP_AFTER >= 2:
                batch_root(0, LN)
                pool.wait_ge(slots_ready, 1)
                pool.wait_ge(zeroed, 32)
                for t in range(TILES):
                    for c in range(2):
                        pool.wait_ge(row_scaled, 2 * t + c + 1)
                        scatter(t, c, 0)
                def hand(t, s, fresh=False):
                    if not fresh:
                        pool.wait_ge(ff_xT_psum, t - 1)
                    g.tensor_copy(xn[:, s, :], z[:, t, :] if isinstance(t, int) else
                                  z[:, bass.ds(t, 1), :].rearrange("p a d -> p (a d)")).then_inc(ff_x_handed, 1)

                hand(0, 0, fresh=True)
                hand(1, 1, fresh=True)
                with pool.Fori(0, TILES // 2 - 1) as i:
                    hand(i * 2 + 2, 0)
                    hand(i * 2 + 3, 1)
                for c in range(2):
                    pool.wait_ge(ff_y_stored[c], SWIGLU.tiles * 8)
                for t in range(TILES):
                    for c in range(2):
                        if t >= 1:
                            pool.wait_ge(row_added, 2 * t + c - 1)
                        gather(t, c, 0)
                end_phase(pool, "pool")

            if STOP_AFTER >= 3:
                begin_phase(pool, "pool", 2)
                batch_root(1, LN)
                end_phase(pool, "pool")
            if STOP_AFTER >= 4:
                begin_phase(pool, "pool", 3)
                batch_root(2, LN)
                pool.wait_ge(dist_in, 32)
                pool.wait_ge(tb_in, 16)
                pool.sem_inc(relu_used, 2)
                time_bias(0, 0, 32)
                end_phase(pool, "pool")
            if STOP_AFTER >= 5:
                begin_phase(pool, "pool", 4)
                batch_root(3, LN)
                def decoder_layer(l):
                    context_attention(TIMED, DECODER, l * 16 + 16, l)
                    end_phase(pool, "pool")
                    begin_phase(pool, "pool", l * 2 + 5)
                    for q in range(GROUPS):
                        pool.wait_ge(gn_var, l * 4 + (q + 1))
                        g.tensor_tensor(rstd[:, 0:4], pow_in[:, 0:4], plus_half[:, 0:4], ALU.pow).then_inc(gn_rstd, 1)
                    end_phase(pool, "pool")

                with pool.Fori(0, LAYERS) as l:
                    decoder_layer(l)
                batch_root(4, DECODER)
                end_phase(pool, "pool")
            if STOP_AFTER >= 6:
                batch_root(5, LN)
                end_phase(pool, "pool")
            if STOP_AFTER >= 7:
                context_attention(SWISH, LN, 80)
                end_phase(pool, "pool")
            if STOP_AFTER >= 8:
                pool.wait_ge(wg_square, 1)
                g.tensor_tensor(wg_col[:, 1:2], wg_col[:, 0:1], plus_half[0:8, 0:1], ALU.pow).then_inc(wg_norm, 1)
                batch_root(6, LN)
                pool.wait_ge(slots_ready, 2)
                for t in range(TILES):
                    g.indirect_dma_start(slots_x[1], bass.IndirectOffsetOnAxis(slot_i[:, 0, t:t + 1], 0),
                                         z[:, t, :], None).then_inc(row_scattered[0], 16)
                for e in range(EXPERTS):
                    pool.wait_ge(gelu_landed[e], 32)
                    pool.sem_inc(experts_in, 1)
                for c in range(2):
                    pool.wait_ge(ff_y_stored[c], (SWIGLU.tiles + GELU.tiles) * 8)
                for t in range(TILES):
                    c = t % 2
                    if t >= 2:
                        pool.wait_ge(row_added, 2 * TILES + t - 1)
                    g.indirect_dma_start(rows_ring[:, c, :], None, slots_y[1],
                                         bass.IndirectOffsetOnAxis(slot_i[:, 0, t:t + 1], 0)).then_inc(row_gathered[c], 16)
                end_phase(pool, "pool")



def layouts(np, i):
    f = lambda v: np.ascontiguousarray(np.asarray(v))
    rows = lambda v: f(v.reshape(v.shape[0] // 128, 128, -1).transpose(1, 0, 2))
    tiles = lambda v: f(v.reshape(2, 8, 128, -1).transpose(2, 1, 0, 3).reshape(128, -1))
    g = {k: np.asarray(v) for k, v in i.items()}
    a = {}
    p = np.arange(128)
    a["ident"] = np.eye(128, dtype=np.float32)
    a["tri"] = np.where(p[None, :] > p[:, None], np.float32(-1e30), np.float32(0)).astype(np.float32)
    a["bd_mask"] = f(np.concatenate([p[:, None] // 16 == np.arange(8)[None], p[:, None] // 64 == np.arange(2)[None]], 1).astype(np.float32))
    e = np.arange(8)
    a["earlier"] = f(np.broadcast_to((e[None, :] < e[:, None]).astype(np.float32).reshape(1, 64), (128, 64)))
    a["later8"] = f(np.broadcast_to((8 - e).astype(np.float32)[None], (128, 8)))
    a["x"] = tiles(g["x"])
    c = g["ctx_1024"].reshape(154, 256).T
    a["ctxT"] = f(rows(c).reshape(128, -1))
    a["mask_keep"] = tiles(g["mask_Bx1xSxS2_ik1"].reshape(2, 1024, 77))
    a["L0_wk"] = rows(g["L0_xattn_Wk"].T)
    a["L0_wv"] = rows(g["L0_xattn_Wv"].T)
    a["L0_wq"] = rows(g["L0_xattn_Wq"])
    a["L0_wo"] = rows(g["L0_xattn_Wo"].T)
    a["before"] = (p[:, None] < p[None, :]).astype(np.float32)
    a["ones"] = np.ones((128, 128), np.float32)
    a["tile_of"] = f(np.broadcast_to(np.arange(SLOT_TILES, dtype=np.float32)[None], (128, SLOT_TILES)))
    experts = lambda v: np.stack([rows(v[k]) for k in range(len(v))])
    w1 = np.concatenate([g["L0_ffn_w1"], g["L0_ffn_w1s"]])
    w3 = np.concatenate([g["L0_ffn_w3"], g["L0_ffn_w3s"]])
    a["L0_w13"] = experts(np.concatenate([w1, w3], 2))
    a["L0_w2"] = experts(np.concatenate([g["L0_ffn_w2"], g["L0_ffn_w2s"]]))
    a["L0_gate"] = rows(g["L0_ffn_gate_w"].T)
    a["L1_Ws"] = rows(g["L1_xattn_Ws"])
    a["L1_W"] = rows(g["L1_xattn_W"])
    col = lambda v: f(v.reshape(-1, 128).T)
    rep = lambda v: f(np.broadcast_to(v.reshape(1, -1), (128, v.size)))
    a["L1_cols"] = f(np.concatenate([col(g["L1_xattn_w"]), col(g["L1_xattn_Wcw"]), col(g["L1_xattn_Wcb"]),
                                     np.zeros((128, 2), np.float32)], 1))
    a["L1_b"] = col(g["L1_xattn_b"])
    a["L1_sb"] = rep(np.concatenate([g["L1_xattn_bcw"], g["L1_xattn_bcb"]]))
    a["q_mask"] = rep(g["mask_BxS2_ik0"])
    a["L1_gate"] = rows(g["L1_ffn_w_gate"])
    qk = np.stack([rows(g["L1_ffn_w_q"]), rows(g["L1_ffn_w_k"])], 2).reshape(128, 2, 2, 4, 128)
    a["L1_wqk"] = f(qk.transpose(3, 0, 1, 2, 4).reshape(4, 128, -1))
    ve = g["L1_ffn_value_experts"]
    a["L1_ve"] = f(ve.reshape(8, 4, 2, 2, 128, 64).transpose(1, 4, 3, 2, 0, 5).reshape(4, 128, -1))
    oe = g["L1_ffn_output_experts"]
    a["L1_oe"] = f(oe.reshape(4, 2, 4, 2, 64, 256).transpose(2, 1, 4, 3, 0, 5).reshape(4, 128, -1))
    a["dist"] = tiles(g["fside_BxSxS2_0"])
    a["ff0"] = rep(g["mask_Bx1x1xS2_ff0"])
    a["tb"] = f(np.broadcast_to(np.concatenate([g["L2_xattn_Wth"].reshape(4, 32), g["L2_xattn_bth"],
                                                g["L2_xattn_Wto"].reshape(4, 32), g["L2_xattn_bto"]], 1)[:, None], (4, 128, 97)))
    per = lambda fn, v: np.stack([fn(v[k]) for k in range(4)])
    a["L2_wk"] = per(lambda v: rows(v.reshape(256, 1024)), g["L2_xattn_Wk"])
    a["L2_wv"] = per(lambda v: rows(v.reshape(256, 1024)), g["L2_xattn_Wv"])
    a["L2_wq"] = per(lambda v: rows(v.reshape(256, 1024).T), g["L2_xattn_Wq"])
    a["L2_wo"] = per(lambda v: rows(v.reshape(1024, 256)), g["L2_xattn_Wo"])
    a["L2_f1"] = per(lambda v: rows(v).reshape(128, -1), g["L2_xattn_Wf1"])
    a["L2_f2"] = per(lambda v: rows(v).reshape(128, -1), g["L2_xattn_Wf2"])
    a["L2_bf1"] = per(col, g["L2_xattn_bf1"])
    a["L2_bf2"] = per(rep, g["L2_xattn_bf2"])
    a["L2_sign"] = rows(g["L2_ffn_weight"].T)
    a["L3_wk"] = rows(g["L3_xattn_key_down"].transpose(1, 0, 2).reshape(256, 512))
    a["L3_wv"] = rows(g["L3_xattn_value_down"].transpose(1, 0, 2).reshape(256, 512))
    a["L3_wq"] = rows(g["L3_xattn_query_down"].transpose(0, 2, 1).reshape(512, 256))
    a["L3_wo"] = rows(g["L3_xattn_value_up"].reshape(512, 256))
    a["L3_qb"] = col(g["L3_xattn_query_down_bias"])
    a["L3_redT"] = f(g["L3_ffn_w_red"].T)
    a["L3_wg"] = f(g["L3_ffn_wg"])
    a["L3_w1"] = experts(g["L3_ffn_w1"])
    a["L3_w2"] = experts(g["L3_ffn_w2"])
    a["L3_b1"] = f(g["L3_ffn_b1"])
    a["L3_b2"] = f(g["L3_ffn_b2"])
    a["bo"] = f(np.broadcast_to(g["L0_xattn_bo"][None], (128, 256)))
    return a


def kernel(**inputs):
    import numpy as np
    import concourse.bacc as bacc
    from concourse import mybir as mb
    from concourse.bass_utils import run_bass_kernel_spmd

    nc = bacc.Bacc("TRN2", target_bir_lowering=False, num_devices=1)
    arrays = layouts(np, inputs)
    aps = {k: nc.dram_tensor("in_" + k, v.shape, mb.dt.from_np(v.dtype), kind="ExternalInput").ap()
           for k, v in arrays.items()}
    out = nc.dram_tensor("out_x", (128, 16 * 256), mb.dt.float32, kind="ExternalOutput").ap()
    megakernel(nc, aps, out)
    r = run_bass_kernel_spmd(nc, [{"in_" + k: v for k, v in arrays.items()}], core_ids=[0])
    y = r.results[0]["out_x"]
    return np.ascontiguousarray(y.reshape(128, 8, 2, 256).transpose(2, 1, 0, 3).reshape(2, 1024, 256))
```
